# Optimizing a Trainium2 kernel written in Bass

```python
import numpy as np
import jax
import jax.numpy as jnp

def _softmax(x, axis=-1):
    return jax.nn.softmax(x, axis=axis)

def _gelu(x):
    return jax.nn.gelu(x, approximate=True)

def _silu(x):
    return jax.nn.silu(x)

def _sigmoid(x):
    return jax.nn.sigmoid(x)

def _layernorm(x, axis=-1, eps=1e-05):
    m = jnp.mean(x, axis=axis, keepdims=True)
    v = jnp.var(x, axis=axis, keepdims=True)
    return (x - m) / jnp.sqrt(v + eps)

def _scatter_add(tgt, idx, src, axis=0):
    return tgt.at[idx].add(src)

def _segment_sum(src, seg, n):
    return jax.ops.segment_sum(src, seg, n)
kernel_name = 'mk_adj_preln_d4_adj_r2_681554'

def setup_inputs(seed: int=0):
    np.random.seed(seed)
    _w = jnp.asarray

    def _rec_inputs():
        import jax
        import jax.numpy as jnp
        _gk = jax.random.key(seed)
        x = -0.000929 + 1 * jax.random.normal(jax.random.fold_in(_gk, 1), (4096, 128), jnp.float32)
        _w = (1.0 + jnp.arange(4096, dtype=jnp.float32)) ** (-0.5)
        _w = _w / _w.mean()
        _pij = jnp.clip(0.000976562 * _w[:, None] * _w[None, :], 0.0, 1.0)
        _a = jax.random.uniform(jax.random.fold_in(_gk, 2), (4096, 4096)) < _pij
        _a = jnp.logical_or(_a, jnp.eye(4096, dtype=bool))
        _af = _a.astype(jnp.float32)
        _af = _af * jax.random.uniform(jax.random.fold_in(_gk, 3), (4096, 4096), jnp.float32, 0.05, 1)
        adj = _af
        return (x, adj)
    x, adj = _rec_inputs()

    def _L0_gnn_setup():
        import jax, jax.numpy as jnp
        import numpy as np
        N = 4096
        F_IN = 128
        F_OUT = 128
        key = jax.random.key(seed)
        k1, k2, k3, k4, k5 = jax.random.split(key, 5)
        x = jax.random.normal(k1, (N, F_IN), dtype=jnp.float32)
        adj = jax.random.uniform(k2, (N, N), dtype=jnp.float32)
        kernel = jax.random.normal(k3, (F_IN, F_OUT), dtype=jnp.float32) * 0.05
        bias = jax.random.normal(k4, (F_OUT,), dtype=jnp.float32) * 0.05
        beta = jax.random.uniform(k5, (N,), dtype=jnp.float32)
        return {'x': x, 'adj': adj, 'kernel': kernel, 'bias': bias, 'beta': beta}
    _L0_gnn_all = _L0_gnn_setup()
    _L0_gnn_in = {k: v for k, v in _L0_gnn_all.items() if k in ('kernel', 'bias', 'beta')}
    del _L0_gnn_all

    def _L1_gnn_setup():
        import jax, jax.numpy as jnp
        import numpy as np
        N = 5000
        D = 128
        DENSITY = 0.003
        key = jax.random.key(seed)
        k1, k2, k3 = jax.random.split(key, 3)
        inputs = jax.random.normal(k1, (N, D), dtype=jnp.float32)
        u = jax.random.uniform(k2, (N, N), dtype=jnp.float32)
        adj = jnp.where(u < DENSITY, u * (1.0 / DENSITY), 0.0) + jnp.eye(N, dtype=jnp.float32)
        H_v = jax.random.normal(k3, (D, 1), dtype=jnp.float32) * 0.1
        return {'inputs': inputs, 'adj': adj, 'H_v': H_v}
    _L1_gnn_all = _L1_gnn_setup()
    _L1_gnn_in = {k: v for k, v in _L1_gnn_all.items() if k in ('H_v',)}
    del _L1_gnn_all

    def _L2_gnn_setup():
        import jax, jax.numpy as jnp
        import numpy as np
        IN_DIM = 128
        OUT_DIM = 128
        N = 8192
        key = jax.random.key(seed)
        k_x, k_adj, k_w, k_b = jax.random.split(key, 4)
        x = jax.random.normal(k_x, (N, IN_DIM), dtype=jnp.float32)
        adj = jax.random.uniform(k_adj, (N, N), dtype=jnp.float32)
        bound = 1.0 / np.sqrt(2 * IN_DIM)
        W = jax.random.uniform(k_w, (OUT_DIM, 2 * IN_DIM), dtype=jnp.float32, minval=-bound, maxval=bound)
        b = jax.random.uniform(k_b, (OUT_DIM,), dtype=jnp.float32, minval=-bound, maxval=bound)
        return {'x': x, 'adj': adj, 'W': W, 'b': b}
    _L2_gnn_all = _L2_gnn_setup()
    _L2_gnn_in = {k: v for k, v in _L2_gnn_all.items() if k in ('W', 'b')}
    del _L2_gnn_all

    def _L3_gnn_setup():
        import jax, jax.numpy as jnp
        import numpy as np
        N, IN, H, C = (2048, 128, 4, 32)
        HC = H * C
        EDGE_P = 0.008

        def _linear_params(key, fan_in, fan_out, bias=True):
            k1, k2 = jax.random.split(key)
            lim = 1.0 / np.sqrt(fan_in)
            W = jax.random.uniform(k1, (fan_in, fan_out), jnp.float32, -lim, lim)
            if not bias:
                return W
            b = jax.random.uniform(k2, (fan_out,), jnp.float32, -lim, lim)
            return (W, b)

        def _transformer_conv(x, adj, Wq, bq, Wk, bk, Wv, bv, Ws, bs, Wb):
            n = x.shape[0]
            q = (x @ Wq + bq).reshape(n, H, C)
            k = (x @ Wk + bk).reshape(n, H, C)
            v = (x @ Wv + bv).reshape(n, H, C)
            attn = jnp.einsum('nhc,mhc->hnm', q, k) / np.float32(np.sqrt(C))
            mask = adj == 0.0
            neg = jnp.where(mask[None], -jnp.inf, attn)
            m = jnp.max(neg, axis=-1, keepdims=True)
            all_inf = jnp.isneginf(m)
            e = jnp.where(mask[None], 0.0, jnp.exp(neg - jnp.where(all_inf, 0.0, m)))
            denom = jnp.sum(e, axis=-1, keepdims=True)
            alpha = e / jnp.where(denom == 0.0, 1.0, denom)
            out = jnp.einsum('hnm,mhc->hnc', alpha, v)
            out = jnp.transpose(out, (1, 2, 0)).reshape(n, C * H)
            x_r = x @ Ws + bs
            beta = jax.nn.sigmoid(jnp.concatenate([out, x_r, out - x_r], axis=-1) @ Wb)
            return beta * x_r + (1.0 - beta) * out
        key = jax.random.key(seed)
        ks = jax.random.split(key, 7)
        x = jax.random.normal(ks[0], (N, IN), jnp.float32)
        adj = (jax.random.uniform(ks[1], (N, N)) < EDGE_P).astype(jnp.float32)
        Wq, bq = _linear_params(ks[2], IN, HC)
        Wk, bk = _linear_params(ks[3], IN, HC)
        Wv, bv = _linear_params(ks[4], IN, HC)
        Ws, bs = _linear_params(ks[5], IN, HC)
        Wb = _linear_params(ks[6], 3 * HC, 1, bias=False)
        return dict(x=x, adj=adj, Wq=Wq, bq=bq, Wk=Wk, bk=bk, Wv=Wv, bv=bv, Ws=Ws, bs=bs, Wb=Wb)
    _L3_gnn_all = _L3_gnn_setup()
    _L3_gnn_in = {k: v for k, v in _L3_gnn_all.items() if k in ('Wq', 'bq', 'Wk', 'bk', 'Wv', 'bv', 'Ws', 'bs', 'Wb')}
    del _L3_gnn_all
    return {'x': x, 'adj': adj, 'L0_gnn_kernel': _L0_gnn_in['kernel'], 'L0_gnn_bias': _L0_gnn_in['bias'], 'L0_gnn_beta': _L0_gnn_in['beta'], 'L1_gnn_H_v': _L1_gnn_in['H_v'], 'L2_gnn_W': _L2_gnn_in['W'], 'L2_gnn_b': _L2_gnn_in['b'], 'L3_gnn_Wq': _L3_gnn_in['Wq'], 'L3_gnn_bq': _L3_gnn_in['bq'], 'L3_gnn_Wk': _L3_gnn_in['Wk'], 'L3_gnn_bk': _L3_gnn_in['bk'], 'L3_gnn_Wv': _L3_gnn_in['Wv'], 'L3_gnn_bv': _L3_gnn_in['bv'], 'L3_gnn_Ws': _L3_gnn_in['Ws'], 'L3_gnn_bs': _L3_gnn_in['bs'], 'L3_gnn_Wb': _L3_gnn_in['Wb']}

def reference(x, adj, L0_gnn_kernel, L0_gnn_bias, L0_gnn_beta, L1_gnn_H_v, L2_gnn_W, L2_gnn_b, L3_gnn_Wq, L3_gnn_bq, L3_gnn_Wk, L3_gnn_bk, L3_gnn_Wv, L3_gnn_bv, L3_gnn_Ws, L3_gnn_bs, L3_gnn_Wb):
    import jax
    import jax.numpy as jnp

    def _L0_gnn_ref(x, adj, kernel, bias, beta):
        import jax, jax.numpy as jnp
        import numpy as np
        N = 4096
        F_IN = 128
        F_OUT = 128
        inv_deg = 1.0 / (jnp.sum(adj, axis=1) + beta)
        agg = adj @ x + beta[:, None] * x
        out = inv_deg[:, None] * agg @ kernel + bias
        return out

    def _L1_gnn_ref(inputs, adj, H_v):
        import jax, jax.numpy as jnp
        import numpy as np
        N = 5000
        D = 128
        DENSITY = 0.003
        score = jnp.squeeze(inputs @ H_v, axis=-1)
        mask = adj != 0.0
        logits = jnp.where(mask, adj * score[None, :], -1e+30)
        weights = jax.nn.softmax(logits, axis=-1)
        output = weights @ inputs
        return output

    def _L2_gnn_ref(x, adj, W, b):
        import jax, jax.numpy as jnp
        import numpy as np
        IN_DIM = 128
        OUT_DIM = 128
        N = 8192
        h_N = jnp.matmul(adj, x)
        h_cat = jnp.concatenate([x, h_N], axis=-1)
        out = jnp.maximum(jnp.einsum('nd,od->no', h_cat, W) + b, 0.0)
        return out

    def _L3_gnn_ref(x, adj, Wq, bq, Wk, bk, Wv, bv, Ws, bs, Wb):
        import jax, jax.numpy as jnp
        import numpy as np
        N, IN, H, C = (2048, 128, 4, 32)
        HC = H * C
        EDGE_P = 0.008

        def _linear_params(key, fan_in, fan_out, bias=True):
            k1, k2 = jax.random.split(key)
            lim = 1.0 / np.sqrt(fan_in)
            W = jax.random.uniform(k1, (fan_in, fan_out), jnp.float32, -lim, lim)
            if not bias:
                return W
            b = jax.random.uniform(k2, (fan_out,), jnp.float32, -lim, lim)
            return (W, b)

        def _transformer_conv(x, adj, Wq, bq, Wk, bk, Wv, bv, Ws, bs, Wb):
            n = x.shape[0]
            q = (x @ Wq + bq).reshape(n, H, C)
            k = (x @ Wk + bk).reshape(n, H, C)
            v = (x @ Wv + bv).reshape(n, H, C)
            attn = jnp.einsum('nhc,mhc->hnm', q, k) / np.float32(np.sqrt(C))
            mask = adj == 0.0
            neg = jnp.where(mask[None], -jnp.inf, attn)
            m = jnp.max(neg, axis=-1, keepdims=True)
            all_inf = jnp.isneginf(m)
            e = jnp.where(mask[None], 0.0, jnp.exp(neg - jnp.where(all_inf, 0.0, m)))
            denom = jnp.sum(e, axis=-1, keepdims=True)
            alpha = e / jnp.where(denom == 0.0, 1.0, denom)
            out = jnp.einsum('hnm,mhc->hnc', alpha, v)
            out = jnp.transpose(out, (1, 2, 0)).reshape(n, C * H)
            x_r = x @ Ws + bs
            beta = jax.nn.sigmoid(jnp.concatenate([out, x_r, out - x_r], axis=-1) @ Wb)
            return beta * x_r + (1.0 - beta) * out
        return _transformer_conv(x, adj, Wq, bq, Wk, bk, Wv, bv, Ws, bs, Wb)
    h = jnp.maximum(_layernorm(x, axis=-1), 0.0)
    x = x + _L0_gnn_ref(h, adj, L0_gnn_kernel, L0_gnn_bias, L0_gnn_beta)
    h = jnp.maximum(_layernorm(x, axis=-1), 0.0)
    x = x + _L1_gnn_ref(h, adj, L1_gnn_H_v)
    h = jnp.maximum(_layernorm(x, axis=-1), 0.0)
    x = x + _L2_gnn_ref(h, adj, L2_gnn_W, L2_gnn_b)
    h = jnp.maximum(_layernorm(x, axis=-1), 0.0)
    x = x + _L3_gnn_ref(h, adj, L3_gnn_Wq, L3_gnn_bq, L3_gnn_Wk, L3_gnn_bk, L3_gnn_Wv, L3_gnn_bv, L3_gnn_Ws, L3_gnn_bs, L3_gnn_Wb)
    return x

_drawn_inputs = setup_inputs


def setup_inputs(seed=0):
    import zlib

    import numpy as np

    out = dict(_drawn_inputs(seed))
    spreads = {}
    factors = {'L2_gnn_b': 3.331,
     'L3_gnn_Wq': 8.0,
     'L3_gnn_bq': 24.098,
     'L3_gnn_Wk': 8.0,
     'L3_gnn_bk': 64.0,
     'L3_gnn_bv': 3.605,
     'L3_gnn_bs': 3.023}
    for name, (base, spread) in spreads.items():
        noise = np.random.default_rng([zlib.crc32(name.encode()), seed]).standard_normal(out[name].shape)
        drawn = base * np.exp(spread * noise) if base else spread * noise
        out[name] = jnp.asarray(drawn.astype(out[name].dtype))
    for name, factor in factors.items():
        out[name] = (out[name] * factor).astype(out[name].dtype)
    return out
```

```python
from contextlib import ExitStack

import numpy as np
import concourse.bass as bass
from concourse import mybir

F32 = mybir.dt.float32
BF16 = mybir.dt.bfloat16
ALU = mybir.AluOpType
ACT = mybir.ActivationFunctionType
AX = mybir.AxisListType

P = 128
N = 4096
T = N // P
NB = 8
BW = N // NB
TB = BW // P
NQ = 4
MQ = T // NQ
H = 4
C = P // H
PW = 2 * P
NP = N // PW
EPS = 1e-5
NEG = -1e30
SCALE = float(np.float32(1.0) / np.float32(np.sqrt(C)))


def build(nc, x, adj, adj_blocks, k0, b0, beta, hv, w2, b2, wq, bq, wkvs, bkvs, wb, out, kv_table):
    ctx = ExitStack()
    with ctx:
        def sb(name, shape, dt=F32):
            return ctx.enter_context(nc.sbuf_tensor(name, shape, dt))

        def sem(name):
            return ctx.enter_context(nc.semaphore(name))

        x_sb = sb("x_sb", [P, T, P])
        h_sb = sb("h_sb", [P, T, P])
        stats = sb("stats", [P, T, 6])
        rstd = sb("rstd", [P, T])
        nmean = sb("nmean", [P, T])
        lnw = sb("lnw", [P, 4, T])
        ident = sb("ident", [P, P])
        ones = sb("ones", [P, P])
        zeros = sb("zeros", [P, P])
        k0_sb = sb("k0_sb", [P, P])
        w2_sb = sb("w2_sb", [P, 2, P])
        hv_sb = sb("hv_sb", [P, 1])
        hvb = sb("hvb", [P, P])
        b0_bc = sb("b0_bc", [P, P])
        b2_bc = sb("b2_bc", [P, P])
        beta_sb = sb("beta_sb", [P, T])
        wq_sb = sb("wq_sb", [P, P])
        bq_sb = sb("bq_sb", [P, 1])
        wkvs_sb = sb("wkvs_sb", [P, 3 * P])
        bkvs_bc = sb("bkvs_bc", [P, 3 * P])
        wb_bc = sb("wb_bc", [P, 3 * P])
        hmask = sb("hmask", [P, H])
        h_t = sb("h_t", [P, 2, P])
        hT = sb("hT", [P, 2, P])
        aggT = sb("aggT", [P, BW])
        work = sb("work", [P, 30 * 1024])

        ring = work[:, 0:4 * 4096].rearrange("p (q m n) -> p q m n", q=NQ, m=MQ)
        selfterm = work[:, 16384:20480].rearrange("p (t f) -> p t f", t=T)
        degp = work[:, 20480:22528].rearrange("p (q n) -> p q n", q=NQ)
        upd = work[:, 22528:23040].rearrange("p (t f) -> p t f", t=TB)
        upd2 = work[:, 23040:23552].rearrange("p (t f) -> p t f", t=TB)
        inv = work[:, 23552:23556]
        rows = work[:, 0:8192].rearrange("p (b m) -> p b m", b=2)
        logit = work[:, 8192:16384].rearrange("p (b m) -> p b m", b=2)
        neg = work[:, 16384:18432].bitcast(BF16)
        score = work[:, 18432:22528]
        probT = work[:, 22528:23552].rearrange("p (b c n) -> p b c n", b=2, c=4)
        mx = work[:, 23552:23554]
        nmx = work[:, 23554:23556]
        den = work[:, 23556:23558]
        rden = work[:, 23558:23560]
        xnew = work[:, 23680:23808]
        S = work[:, 0:16384].rearrange("p (j h m) -> p j h m", j=NP, h=H)
        vstore = work[:, 16384:20480].rearrange("p (j c f) -> p j c f", j=NP, c=2)
        qT = work[:, 20480:24576]
        kvg = work[:, 24576:25088].rearrange("p (c f) -> p c f", c=2)
        mrow = work[:, 25088:25344]
        mneg = work[:, 25344:25600]
        kT = work[:, 25600:25856]
        qz = work[:, 25856:26368].rearrange("p (h n) -> p h n", h=H)
        e = work[:, 26368:27392].rearrange("p (h m) -> p h m", h=H)
        eT = work[:, 27392:28416].rearrange("p (c h n) -> p c h n", c=2, h=H)
        vs = work[:, 28416:28672].rearrange("p (c f) -> p c f", c=2)
        kvrow = work[:, 28672:29184].rearrange("p (b f) -> p b f", b=2)
        outT = work[:, 29184:29312]
        o = work[:, 29312:29440]
        dif = work[:, 29440:29568]
        junk = work[:, 29568:29696]
        fin = work[:, 29696:29824]
        sm = work[:, 29824:29952]
        xr = h_sb

        ps = ctx.enter_context(nc.psum_tensor("ps", [P, 8, 512], F32))

        ld = sem("ld")
        cst = sem("cst")
        chain = sem("chain")
        block = ctx.enter_context(nc.Block())

        stat_done = [sem(f"stat_done{k}") for k in range(4)]
        ln_ready = [sem(f"ln_ready{k}") for k in range(4)]
        var_ready = [sem(f"var_ready{k}") for k in range(4)]
        std_ready = [sem(f"std_ready{k}") for k in range(4)]
        ht_ready = [sem(f"ht_ready{k}") for k in range(4)]
        ht_copied = [sem(f"ht_copied{k}") for k in range(4)]
        tr_done = [sem(f"tr_done{k}") for k in range(4)]
        hT_ready = [sem(f"hT_ready{k}") for k in range(4)]
        proj_done = [sem(f"proj_done{k}") for k in range(4)]
        post_done = [sem(f"post_done{k}") for k in range(4)]
        slot_full = {k: [sem(f"slot_full{k}_{q}") for q in range(NQ)] for k in (0, 2)}
        slot_used = {k: [sem(f"slot_used{k}_{q}") for q in range(NQ)] for k in (0, 2)}
        slot_summed = [sem(f"slot_summed{q}") for q in range(NQ)]
        agg_done = {k: sem(f"agg_done{k}") for k in (0, 2)}
        agg_out = {k: sem(f"agg_out{k}") for k in (0, 2)}
        up_done = {k: sem(f"up_done{k}") for k in (0, 2)}
        up_used = {k: sem(f"up_used{k}") for k in (0, 2)}
        deg_done = sem("deg_done")
        row_full = [sem("row_full0"), sem("row_full1")]
        prod_ready = sem("prod_ready")
        neg_ready = sem("neg_ready")
        lg_ready = sem("lg_ready")
        e_ready = sem("e_ready")
        pT_done = sem("pT_done")
        pT_out = sem("pT_out")
        pv_grp = sem("pv_grp")
        pv_tile = sem("pv_tile")
        pv_used = sem("pv_used")
        kv_stored = [sem("kv_stored0"), sem("kv_stored1")]
        qz_ready = sem("qz_ready")
        g_full = sem("g_full")
        kT_done = sem("kT_done")
        kT_out = sem("kT_out")
        v_kept = sem("v_kept")
        m_used = sem("m_used")
        s_done = sem("s_done")
        s_out = sem("s_out")
        max_ready = sem("max_ready")
        ex_ready = sem("ex_ready")
        sum_used = sem("sum_used")
        eT_done = sem("eT_done")
        eT_act = sem("eT_act")
        eT_dve = sem("eT_dve")
        vs_ready = sem("vs_ready")
        pv3_pair = sem("pv3_pair")
        pv3_tile = sem("pv3_tile")
        oT_out = sem("oT_out")
        o_done = sem("o_done")
        o_used = sem("o_used")
        z_ready = sem("z_ready")
        ez_ready = sem("ez_ready")
        fin_ready = sem("fin_ready")
        fin_out = sem("fin_out")

        primed = [agg_out[0], agg_out[2], up_used[0], up_used[2], up_done[0], up_done[2], deg_done, kT_done,
                  kT_out, v_kept, m_used, s_done, s_out, eT_done, sum_used, pv3_pair, eT_act, eT_dve, oT_out,
                  o_done, o_used]

        link_ln = [sem(f"link_ln{k}") for k in range(4)]
        link_x = sem("link_x")
        link_up = {k: sem(f"link_up{k}") for k in (0, 2)}
        link_1 = sem("link_1")
        link_1f = sem("link_1f")
        link_3a = sem("link_3a")
        link_3s = sem("link_3s")
        link_3e = sem("link_3e")
        hvb_ready = sem("hvb_ready")
        NLD = 16

        def wait(eng, s, value):
            if isinstance(value, int) and value <= 0:
                return
            eng.wait_ge(s, value)

        def settle(eng):
            eng.nop(nofuse=True)

        def each_tile(eng, body, n=T):
            body(0, 0)
            body(1, 1)
            with eng.Fori(1, n // 2) as i:
                body(2 * i, 0)
                body(2 * i + 1, 1)

        class Link:
            def __init__(self, dve, s, per, turn=0):
                self.dve, self.s, self.per, self.base, self.n = dve, s, per, per * turn, 0

            def __call__(self, ins):
                self.n += 1
                assert self.n <= self.per
                ins.then_inc(self.s, 1)
                self.dve.wait_ge(self.s, self.base + self.n)
                settle(self.dve)

            def end(self):
                assert self.n == self.per, self.n

        @block.sync
        def _(sp):
            sp.dma_start(x_sb[:, :, :], x.rearrange("(t p) f -> p t f", p=P)).then_inc(ld, 16)
            for dst, src in ((k0_sb[:, :], k0), (w2_sb[:, :, :], w2.rearrange("(a f) o -> f a o", a=2)),
                             (hv_sb[:, :], hv), (beta_sb[:, :], beta.rearrange("(t p) -> p t", p=P)),
                             (wq_sb[:, :], wq), (bq_sb[:, :], bq.rearrange("(p a) -> p a", a=1)),
                             (b0_bc[:, :], b0.rearrange("(a f) -> a f", a=1).to_broadcast([P, P])),
                             (b2_bc[:, :], b2.rearrange("(a f) -> a f", a=1).to_broadcast([P, P])),
                             (wb_bc[:, :], wb.rearrange("f a -> a f").to_broadcast([P, 3 * P]))):
                with nc.allow_non_contiguous_dma(reason="small constants"):
                    sp.dma_start(dst, src).then_inc(ld, 16)
            for j, (w, b) in enumerate(zip(wkvs, bkvs)):
                sp.dma_start(wkvs_sb[:, j * P:(j + 1) * P], w).then_inc(ld, 16)
                sp.dma_start(bkvs_bc[:, j * P:(j + 1) * P],
                             b.rearrange("(a f) -> a f", a=1).to_broadcast([P, P])).then_inc(ld, 16)

            def stream(k):
                for q in range(NQ):
                    if k == 2:
                        sp.wait_ge(pv_used, T)
                    sp.dma_start(ring[:, q, :, :], adj_blocks[q, :, :]
                                 .rearrange("p (m n) -> p m n", m=MQ)).then_inc(slot_full[k][q], 16)
                with sp.Fori(1, NB) as nb:
                    for q in range(NQ):
                        sp.wait_ge(slot_used[k][q] if q < NQ - 1 else agg_done[k], nb)
                        if k == 0:
                            sp.wait_ge(slot_summed[q], nb)
                        sp.dma_start(ring[:, q, :, :], adj_blocks[bass.ds(nb * NQ + q, 1), :, :]
                                     .rearrange("a p (m n) -> p (a m) n", m=MQ)).then_inc(slot_full[k][q], 16)

            stream(0)
            sp.wait_ge(up_used[0], 1 + NB)
            for b in range(2):
                sp.dma_start(rows[:, b, :], adj[b * P:(b + 1) * P, :]).then_inc(row_full[b], 16)
            with sp.Fori(1, T // 2) as i:
                for b in range(2):
                    sp.wait_ge(prod_ready, 2 * i + b - 1)
                    sp.wait_ge(neg_ready, 2 * i + b - 1)
                    sp.dma_start(rows[:, b, :], adj[bass.ds((2 * i + b) * P, P), :]).then_inc(row_full[b], 16)
            stream(2)
            with sp.Fori(0, T // 2) as i:
                for b in range(2):
                    sp.wait_ge(post_done[3], 2 * i + b + 1)
                    sp.dma_start(kv_table[bass.ds((2 * i + b) * P, P), :], kvrow[:, b, :]).then_inc(kv_stored[b], 16)
            for b in range(2):
                sp.wait_ge(kv_stored[b], 16 * (T // 2))
            def load_pairs(t):
                with sp.Fori(0, NP) as j:
                    g = t * NP + j
                    sp.wait_ge(kT_done, 1 + g)
                    sp.wait_ge(v_kept, 1 + g)
                    sp.wait_ge(m_used, 1 + g)
                    sp.dma_start(kvg[:, :, :], kv_table[bass.ds(j * PW, PW), :]
                                 .rearrange("(c p) f -> p c f", p=P)).then_inc(g_full, 16)
                    sp.dma_start(mrow[:, :], adj[bass.ds(t * P, P), bass.ds(j * PW, PW)]).then_inc(g_full, 16)

            def store(t):
                sp.wait_ge(fin_ready, t + 1)
                sp.dma_start(out[bass.ds(t * P, P), :], x_sb[:, t, :]).then_inc(fin_out, 16)

            load_pairs(0)
            with sp.Fori(1, T) as t:
                load_pairs(t)
                store(t - 1)
            store(T - 1)
            sp.wait_ge(fin_out, 16 * T)

        @block.gpsimd
        def _(pool):
            for s in primed:
                pool.sem_inc(s, 1)
            nc.gpsimd.memset(ident[:, :], 0.0).then_inc(cst, 1)
            nc.gpsimd.memset(ones[:, :], 1.0).then_inc(cst, 1)
            nc.gpsimd.memset(zeros[:, :], 0.0).then_inc(cst, 1)
            nc.gpsimd.memset(hmask[:, :], 1.0).then_inc(cst, 1)
            pool.wait_ge(cst, 4)
            nc.gpsimd.affine_select(out=ident[:, :], in_=ident[:, :], compare_op=ALU.not_equal, fill=1.0,
                                    base=0, pattern=[[-1, P]], channel_multiplier=1).then_inc(cst, 1)
            nc.gpsimd.affine_select(out=hmask[:, :], in_=hmask[:, :], compare_op=ALU.is_ge, fill=0.0,
                                    base=0, pattern=[[-C, H]], channel_multiplier=1).then_inc(cst, 1)
            pool.wait_ge(cst, 6)
            nc.gpsimd.affine_select(out=hmask[:, :], in_=hmask[:, :], compare_op=ALU.is_ge, fill=0.0,
                                    base=C - 1, pattern=[[C, H]], channel_multiplier=-1).then_inc(cst, 1)

            pool.wait_ge(post_done[1], T)

            def product(t, b):
                pool.wait_ge(row_full[b], 16 * ((t - b) // 2 + 1) if isinstance(t, int) else 8 * (t - b) + 16)
                wait(pool, pT_done, 8 * (t - 1))
                nc.gpsimd.tensor_tensor(logit[:, b, :], rows[:, b, :], score[:, :], ALU.mult).then_inc(prod_ready, 1)

            each_tile(pool, product)
            with pool.Fori(0, T) as t:
                with pool.Fori(0, NP) as j:
                    g = t * NP + j
                    pool.wait_ge(g_full, 32 * g + 32)
                    nc.gpsimd.tensor_copy(vstore[:, bass.ds(j, 1), :, :].rearrange("p a c f -> p (a c) f"),
                                          kvg[:, :, P:2 * P]).then_inc(v_kept, 1)
                pool.wait_ge(v_kept, 1 + t * NP + NP)
                settle(pool)
                with pool.Fori(0, NP) as j:
                    g = t * NP + j
                    pool.wait_ge(pv3_pair, 1 + g)
                    nc.gpsimd.tensor_copy(vs[:, :, :], vstore[:, bass.ds(j, 1), :, :]
                                          .rearrange("p a c f -> p (a c) f")).then_inc(vs_ready, 1)

        @block.scalar
        def _(act):
            def normalise(k):
                act.wait_ge(var_ready[k], 1)
                nc.scalar.activation(lnw[:, 3, :], lnw[:, 2, :], ACT.Sqrt).then_inc(std_ready[k], 1)
                act.wait_ge(ln_ready[k], 1)

                def relu(t, b):
                    wait(act, tr_done[k], t - 1)
                    if k < 3:
                        wait(act, ht_copied[k], t - 1)
                    nc.scalar.activation(h_t[:, b, :], x_sb[:, t, :], ACT.Relu, bias=nmean[:, bass.ds(t, 1)],
                                         scale=rstd[:, bass.ds(t, 1)]).then_inc(ht_ready[k], 1)
                each_tile(act, relu)

            def aggregate(k):
                with act.Fori(0, NB) as nb:
                    act.wait_ge(agg_done[k], nb + 1)
                    act.wait_ge(up_done[k], 1 + nb)
                    nc.scalar.activation(aggT[:, :], ps[:, 0, :], ACT.Copy).then_inc(agg_out[k], 1)

            normalise(0)
            aggregate(0)
            normalise(1)

            def exps(t, b):
                act.wait_ge(lg_ready, t + 1)
                wait(act, pv_used, t - 1)
                nc.scalar.activation(logit[:, b, :], logit[:, b, :], ACT.Exp, bias=nmx[:, b:b + 1],
                                     accum_out=den[:, b:b + 1]).then_inc(e_ready, 1)

            def turn(t, lo, hi):
                for n in range(lo, hi):
                    act.wait_ge(pT_done, 8 * t + n + 1)
                    wait(act, pv_grp, 8 * t + n - 1)
                    nc.scalar.activation(probT[:, n % 2, :, :], ps[:, n % 2, :]
                                         .rearrange("p (c n) -> p c n", c=4), ACT.Copy).then_inc(pT_out, 1)

            def layer1(t, b):
                turn(t, 0, 4)
                exps(t + 1, 1 - b)
                turn(t, 4, 8)

            exps(0, 0)
            layer1(0, 0)
            layer1(1, 1)
            with act.Fori(1, T // 2 - 1) as i:
                layer1(2 * i, 0)
                layer1(2 * i + 1, 1)
            layer1(T - 2, 0)
            turn(T - 1, 0, 8)

            normalise(2)
            aggregate(2)
            normalise(3)

            with act.Fori(0, T) as t:
                with act.Fori(0, NP) as j:
                    g = t * NP + j
                    act.wait_ge(kT_done, g + 2)
                    act.wait_ge(s_done, 1 + 2 * g)
                    nc.scalar.activation(kT[:, :], ps[:, 0, 0:PW], ACT.Copy).then_inc(kT_out, 1)
                act.wait_ge(max_ready, t + 1)
                with act.Fori(0, NP) as j:
                    g = t * NP + j
                    act.wait_ge(eT_done, 1 + 2 * g)
                    act.wait_ge(sum_used, 1 + g)
                    for h in range(H):
                        ins = nc.scalar.activation(e[:, h, :], S[:, bass.ds(j, 1), h, :].rearrange("p a m -> p (a m)"),
                                                   ACT.Exp, bias=sm[:, 8 + h:9 + h], scale=SCALE,
                                                   accum_out=sm[:, 12 + h:13 + h])
                    ins.then_inc(ex_ready, 1)
                    act.wait_ge(eT_done, 2 * g + 2)
                    act.wait_ge(pv3_pair, 1 + g)
                    nc.scalar.activation(eT[:, 0, :, :], ps[:, 3, :].rearrange("p (h n) -> p h n", h=H),
                                         ACT.Copy).then_inc(eT_act, 1)
                act.wait_ge(pv3_tile, t + 1)
                act.wait_ge(o_done, 1 + t)
                nc.scalar.activation(outT[:, :], ps[:, 5, 0:P], ACT.Copy).then_inc(oT_out, 1)
                act.wait_ge(z_ready, t + 1)
                nc.scalar.activation(sm[:, 41:42], sm[:, 40:41], ACT.Exp, scale=-1.0).then_inc(ez_ready, 1)

        @block.vector
        def _(dve):
            dve.wait_ge(ld, 16 * NLD)
            dve.wait_ge(cst, 7)
            nc.vector.tensor_scalar(hvb[:, :], ones[:, :], hv_sb[:, 0:1], None, ALU.mult).then_inc(hvb_ready, 1)

            def row_stats(k, nb):
                for j in range(TB):
                    ins = nc.vector.bn_stats(stats[:, TB * nb + j, :], x_sb[:, TB * nb + j, :])
                ins.then_inc(stat_done[k], 1)

            def moments(k, count):
                dve.wait_ge(stat_done[k], count)
                link = Link(dve, link_ln[k], 8)
                a, d, v, sd = (lnw[:, n, :] for n in range(4))
                me, mo, ve, vo = (stats[:, :, n] for n in (1, 4, 2, 5))
                link(nc.vector.tensor_tensor(d, me, mo, ALU.subtract))
                link(nc.vector.tensor_tensor(a, ve, vo, ALU.add))
                link(nc.vector.tensor_tensor(d, d, d, ALU.mult))
                link(nc.vector.tensor_scalar(a, a, 1.0 / P, EPS, ALU.mult, ALU.add))
                link(nc.vector.scalar_tensor_tensor(v, d, 0.25, a, ALU.mult, ALU.add))
                nc.vector.tensor_tensor(a, me, mo, ALU.add).then_inc(var_ready[k], 1)
                dve.wait_ge(var_ready[k], 1)
                dve.wait_ge(std_ready[k], 1)
                link(nc.vector.reciprocal(rstd[:, :], sd))
                link(nc.vector.scalar_tensor_tensor(nmean[:, :], a, -0.5, rstd[:, :], ALU.mult, ALU.mult))
                link(nc.vector.tensor_copy(lnw[:, 1, :], rstd[:, :]))
                link.end()
                nc.vector.tensor_copy(lnw[:, 0, :], nmean[:, :]).then_inc(ln_ready[k], 1)

            def node_terms(k):
                def tile(t, b):
                    dve.wait_ge(ht_ready[k], t + 1)
                    if k < 3:
                        nc.vector.tensor_copy(h_sb[:, t, :], h_t[:, b, :]).then_inc(ht_copied[k], 1)
                    dve.wait_ge(tr_done[k], t + 1)
                    wait(dve, proj_done[k], t - 1)
                    nc.vector.tensor_copy(hT[:, b, :], ps[:, b, 0:P]).then_inc(hT_ready[k], 1)
                    dve.wait_ge(proj_done[k], t + 1)
                    got = ps[:, 2 + b, 0:P]
                    if k == 0:
                        ins = nc.vector.tensor_scalar(selfterm[:, t, :], got, beta_sb[:, bass.ds(t, 1)], None, ALU.mult)
                    elif k == 1:
                        ins = nc.vector.tensor_copy(score[:, bass.ds(t * P, P)], got)
                    elif k == 2:
                        ins = nc.vector.tensor_tensor(selfterm[:, t, :], got, b2_bc[:, :], ALU.add)
                    else:
                        if not isinstance(t, int):
                            dve.wait_ge(kv_stored[b], 8 * (t - b))
                        nc.vector.tensor_tensor(kvrow[:, b, :], ps[:, 2 + b, 0:2 * P], bkvs_bc[:, 0:2 * P], ALU.add)
                        nc.vector.tensor_tensor(xr[:, t, :], ps[:, 2 + b, 2 * P:3 * P], bkvs_bc[:, 2 * P:3 * P], ALU.add)
                        ins = nc.vector.tensor_scalar(qT[:, bass.ds(t * P, P)], ps[:, 4 + b, 0:P], bq_sb[:, 0:1],
                                                      None, ALU.add)
                    ins.then_inc(post_done[k], 1)
                each_tile(dve, tile)

            def update(k):
                with dve.Fori(0, NB) as nb:
                    link = Link(dve, link_up[k], 5 if k == 0 else 2, nb)
                    xs = x_sb[:, bass.ds(nb * TB, TB), :]
                    own = selfterm[:, bass.ds(nb * TB, TB), :]
                    got = ps[:, 1, :].rearrange("p (t f) -> p t f", t=TB)
                    if k == 0:
                        for q in range(NQ):
                            dve.wait_ge(slot_full[k][q], 16 * nb + 16)
                            if q == 0:
                                dve.wait_ge(deg_done, 1 + nb)
                            nc.vector.tensor_reduce(degp[:, q, :], ring[:, q, :, :].rearrange("p m n -> p n m"),
                                                    AX.X, ALU.add).then_inc(slot_summed[q], 1)
                        dve.wait_ge(deg_done, nb + 2)
                        link(nc.vector.tensor_tensor(inv, ps[:, 6, 0:TB], beta_sb[:, bass.ds(nb * TB, TB)], ALU.add))
                        link(nc.vector.reciprocal(inv, inv))
                        dve.wait_ge(up_done[k], nb + 2)
                        nc.vector.tensor_tensor(upd, got, own, ALU.add).then_inc(up_used[k], 1)
                        dve.wait_ge(up_used[k], nb + 2)
                        link(nc.vector.tensor_tensor(upd2, upd, inv.rearrange("p (t a) -> p t a", a=1)
                                                     .to_broadcast([P, TB, P]), ALU.mult))
                        link(nc.vector.tensor_tensor(upd, upd2, b0_bc[:, :].rearrange("p (a f) -> p a f", a=1)
                                                     .to_broadcast([P, TB, P]), ALU.add))
                        link(nc.vector.tensor_tensor(xs, upd, xs, ALU.add))
                    else:
                        dve.wait_ge(up_done[k], nb + 2)
                        nc.vector.tensor_tensor(upd, got, own, ALU.add).then_inc(up_used[k], 1)
                        dve.wait_ge(up_used[k], nb + 2)
                        link(nc.vector.tensor_scalar(upd2, upd, 0.0, None, ALU.max))
                        link(nc.vector.tensor_tensor(xs, upd2, xs, ALU.add))
                    link.end()
                    row_stats(k + 1, nb)

            with dve.Fori(0, NB) as nb:
                row_stats(0, nb)
            moments(0, NB)
            node_terms(0)
            update(0)
            moments(1, NB)
            node_terms(1)

            def mask_and_max(t, b):
                dve.wait_ge(row_full[b], 16 * (t // 2) + 16 if isinstance(t, int) else 8 * (t - b) + 16)
                nc.vector.tensor_scalar(neg, rows[:, b, :], 0.0, NEG, ALU.is_equal, ALU.mult).then_inc(neg_ready, 1)
                dve.wait_ge(neg_ready, t + 1)
                dve.wait_ge(prod_ready, t + 1)
                wait(dve, e_ready, t - 1)
                settle(dve)
                link = Link(dve, link_1, 1, t)
                link(nc.vector.tensor_tensor_reduce(out=logit[:, b, :], in0=logit[:, b, :], in1=neg, scale=1.0,
                                                    scalar=-3.0e38, op0=ALU.add, op1=ALU.max,
                                                    accum_out=mx[:, b:b + 1]))
                link.end()
                nc.vector.tensor_scalar(nmx[:, b:b + 1], mx[:, b:b + 1], -1.0, None, ALU.mult).then_inc(lg_ready, 1)

            def mean_and_add(t, b):
                link = Link(dve, link_1f, 2, t)
                dve.wait_ge(e_ready, t + 1)
                link(nc.vector.reciprocal(rden[:, b:b + 1], den[:, b:b + 1]))
                dve.wait_ge(pv_grp, 8 * t + 8)
                link(nc.vector.scalar_tensor_tensor(xnew, ps[:, 4 + b, 0:P], rden[:, b:b + 1],
                                                    x_sb[:, t, :], ALU.mult, ALU.add))
                link.end()
                nc.vector.tensor_copy(x_sb[:, t, :], xnew).then_inc(pv_used, 1)
                nc.vector.bn_stats(stats[:, t, :], xnew).then_inc(stat_done[2], 1)

            mask_and_max(0, 0)
            mask_and_max(1, 1)
            mean_and_add(0, 0)
            with dve.Fori(1, T // 2) as i:
                mask_and_max(2 * i, 0)
                mean_and_add(2 * i - 1, 1)
                mask_and_max(2 * i + 1, 1)
                mean_and_add(2 * i, 0)
            mean_and_add(T - 1, 1)
            moments(2, T)
            node_terms(2)
            update(2)
            moments(3, NB)
            node_terms(3)

            pmax, rmax, nmax, part, total = (sm[:, 4 * n:4 * n + 4] for n in range(5))
            some, rl = sm[:, 20:24], sm[:, 24:28]
            z = [sm[:, 38:39], sm[:, 39:40], sm[:, 40:41]]
            ez, nb_ = sm[:, 41:42], sm[:, 42:43]
            with dve.Fori(0, T) as t:
                link = Link(dve, link_3s, 14, t)
                nc.vector.memset(rmax, -3.0e38)
                nc.vector.memset(total, 0.0)
                nc.vector.tensor_tensor(qz[:, :, :], qT[:, bass.ds(t * P, P)].rearrange("p (a n) -> p a n", a=1)
                                        .to_broadcast([P, H, P]), hmask[:, :].rearrange("p (h a) -> p h a", a=1)
                                        .to_broadcast([P, H, P]), ALU.mult).then_inc(qz_ready, 1)
                dve.wait_ge(qz_ready, t + 1)
                settle(dve)
                with dve.Fori(0, NP) as j:
                    g = t * NP + j
                    step = Link(dve, link_3a, 2, g)
                    dve.wait_ge(g_full, 32 * g + 32)
                    nc.vector.tensor_scalar(mneg[:, :], mrow[:, :], 0.0, NEG, ALU.is_equal, ALU.mult).then_inc(m_used, 1)
                    dve.wait_ge(m_used, g + 2)
                    for f in range(2):
                        dve.wait_ge(s_done, 2 * g + f + 2)
                        nc.vector.tensor_tensor(S[:, bass.ds(j, 1), 2 * f:2 * f + 2, :].rearrange("p a h m -> p (a h) m"),
                                                ps[:, 1 + f, :].rearrange("p (h m) -> p h m", h=2),
                                                mneg[:, :].rearrange("p (a m) -> p a m", a=1).to_broadcast([P, 2, PW]),
                                                ALU.add).then_inc(s_out, 1)
                    dve.wait_ge(s_out, 1 + 2 * g + 2)
                    settle(dve)
                    step(nc.vector.tensor_reduce(pmax, S[:, bass.ds(j, 1), :, :].rearrange("p a h m -> p (a h) m"),
                                                 AX.X, ALU.max))
                    step(nc.vector.tensor_tensor(rmax, rmax, pmax, ALU.max))
                    step.end()
                nc.vector.tensor_scalar(nmax, rmax, -SCALE, None, ALU.mult).then_inc(max_ready, 1)
                link(nc.vector.tensor_scalar(some, rmax, 0.5 * NEG, None, ALU.is_gt))
                with dve.Fori(0, NP) as j:
                    g = t * NP + j
                    dve.wait_ge(ex_ready, g + 1)
                    nc.vector.tensor_tensor(total, total, part, ALU.add).then_inc(sum_used, 1)
                    dve.wait_ge(eT_done, 1 + 2 * g + 2)
                    dve.wait_ge(pv3_pair, 1 + g)
                    nc.vector.tensor_copy(eT[:, 1, :, :], ps[:, 4, :].rearrange("p (h n) -> p h n", h=H)).then_inc(eT_dve, 1)
                dve.wait_ge(sum_used, 1 + t * NP + NP)
                link(nc.vector.reciprocal(rl, total))
                link(nc.vector.tensor_tensor(rl, rl, some, ALU.mult))
                link(nc.vector.tensor_copy(fin[:, :], xr[:, t, :]))
                dve.wait_ge(o_done, t + 2)
                nc.vector.tensor_tensor(o[:, :].rearrange("p (c h) -> p h c", h=H),
                                        ps[:, 6, 0:P].rearrange("p (h c) -> p h c", h=H),
                                        rl.rearrange("p (h a) -> p h a", a=1).to_broadcast([P, H, C]),
                                        ALU.mult).then_inc(o_used, 1)
                dve.wait_ge(o_used, t + 2)
                link(nc.vector.tensor_tensor(dif[:, :], o[:, :], fin[:, :], ALU.subtract))
                for n, v in enumerate((o, fin, dif)):
                    ins = nc.vector.tensor_tensor_reduce(out=junk[:, :], in0=v[:, :], in1=wb_bc[:, n * P:(n + 1) * P],
                                                         scale=1.0, scalar=z[n - 1] if n else 0.0, op0=ALU.mult,
                                                         op1=ALU.add, accum_out=z[n])
                    if n < 2:
                        link(ins)
                ins.then_inc(z_ready, 1)
                dve.wait_ge(ez_ready, t + 1)
                link(nc.vector.tensor_scalar(ez, ez, -1.0, -1.0, ALU.mult, ALU.add))
                link(nc.vector.reciprocal(nb_, ez))
                link(nc.vector.scalar_tensor_tensor(junk[:, :], dif[:, :], nb_, o[:, :], ALU.mult, ALU.add))
                link(nc.vector.tensor_copy(fin[:, :], x_sb[:, t, :]))
                link(nc.vector.tensor_tensor(fin[:, :], fin[:, :], junk[:, :], ALU.add))
                link(nc.vector.tensor_copy(x_sb[:, t, :], fin[:, :]))
                link(nc.vector.memset(junk[:, 0:1], 0.0))
                link.end()
                nc.vector.memset(junk[:, 0:1], 0.0).then_inc(fin_ready, 1)

        @block.tensor
        def _(pe):
            mm = nc.tensor.matmul
            pe.wait_ge(cst, 7)
            pe.wait_ge(ld, 16 * NLD)
            pe.wait_ge(hvb_ready, 1)

            def project(k):
                def tile(t, b):
                    pe.wait_ge(ht_ready[k], t + 1)
                    wait(pe, hT_ready[k], t - 1)
                    nc.tensor.transpose(ps[:, b, 0:P], h_t[:, b, :], ident[:, :]).then_inc(tr_done[k], 1)
                    pe.wait_ge(hT_ready[k], t + 1)
                    wait(pe, post_done[k], t - 1)
                    got = ps[:, 2 + b, 0:P]
                    if k == 0:
                        ins = mm(got, hT[:, b, :], k0_sb[:, :], start=True, stop=True)
                    elif k == 1:
                        ins = mm(got, hvb[:, :], hT[:, b, :], start=True, stop=True)
                    elif k == 2:
                        ins = mm(got, hT[:, b, :], w2_sb[:, 0, :], start=True, stop=True)
                    else:
                        mm(ps[:, 2 + b, 0:3 * P], hT[:, b, :], wkvs_sb[:, :], start=True, stop=True)
                        ins = mm(ps[:, 4 + b, 0:P], wq_sb[:, :], hT[:, b, :], start=True, stop=True)
                    ins.then_inc(proj_done[k], 1)
                each_tile(pe, tile)

            def aggregate(k):
                pe.wait_ge(ht_copied[k], T)
                pe.wait_ge(post_done[k], T)
                with pe.Fori(0, NB) as nb:
                    pe.wait_ge(agg_out[k], 1 + nb)
                    for q in range(NQ):
                        pe.wait_ge(slot_full[k][q], 16 * nb + 16)
                        for m in range(MQ):
                            ins = mm(ps[:, 0, :], h_sb[:, q * MQ + m, :], ring[:, q, m, :],
                                     start=(q + m == 0), stop=(q * MQ + m == T - 1))
                        if q < NQ - 1:
                            ins.then_inc(slot_used[k][q], 1)
                    ins.then_inc(agg_done[k], 1)
                    pe.wait_ge(up_used[k], 1 + nb)
                    if k == 0:
                        for q in range(NQ):
                            pe.wait_ge(slot_summed[q], nb + 1)
                        for j in range(TB):
                            for q in range(NQ):
                                ins = mm(ps[:, 6, j:j + 1], degp[:, q, j * P:(j + 1) * P], ones[:, 0:1],
                                         start=(q == 0), stop=(q == NQ - 1))
                        ins.then_inc(deg_done, 1)
                    pe.wait_ge(agg_out[k], nb + 2)
                    for j in range(TB):
                        ins = mm(ps[:, 1, j * P:(j + 1) * P], aggT[:, j * P:(j + 1) * P],
                                 k0_sb[:, :] if k == 0 else w2_sb[:, 1, :], start=True, stop=True)
                    ins.then_inc(up_done[k], 1)

            project(0)
            aggregate(0)
            project(1)

            def transposes(t, b, n):
                if n == 0:
                    pe.wait_ge(e_ready, t + 1)
                wait(pe, pT_out, 8 * t + n - 1)
                for c in range(4):
                    m = 4 * n + c
                    ins = nc.tensor.transpose(ps[:, n % 2, c * P:(c + 1) * P], logit[:, b, m * P:(m + 1) * P], ident[:, :])
                ins.then_inc(pT_done, 1)

            def weighted(t, b, n):
                if n == 0:
                    wait(pe, pv_used, t - 1)
                pe.wait_ge(pT_out, 8 * t + n + 1)
                for c in range(4):
                    m = 4 * n + c
                    ins = mm(ps[:, 4 + b, 0:P], probT[:, n % 2, c, :], h_sb[:, m, :], start=(m == 0), stop=(m == T - 1))
                ins.then_inc(pv_grp, 1)

            def layer1(t, b):
                transposes(t, b, 0)
                for n in range(8):
                    if n < 7:
                        transposes(t, b, n + 1)
                    weighted(t, b, n)

            pe.wait_ge(ht_copied[1], T)
            pe.wait_ge(post_done[1], T)
            each_tile(pe, layer1)

            project(2)
            aggregate(2)
            project(3)

            with pe.Fori(0, T) as t:
                pe.wait_ge(qz_ready, t + 1)
                settle(pe)
                with pe.Fori(0, NP) as j:
                    g = t * NP + j
                    pe.wait_ge(g_full, 32 * g + 32)
                    pe.wait_ge(kT_out, 1 + g)
                    for c in range(2):
                        ins = nc.tensor.transpose(ps[:, 0, c * P:(c + 1) * P], kvg[:, c, 0:P], ident[:, :])
                    ins.then_inc(kT_done, 1)
                    pe.wait_ge(kT_out, g + 2)
                    pe.wait_ge(s_out, 1 + 2 * g)
                    for f in range(2):
                        for u in range(2):
                            ins = mm(ps[:, 1 + f, u * PW:(u + 1) * PW], qz[:, 2 * f + u, :], kT[:, :], start=True, stop=True)
                        ins.then_inc(s_done, 1)
                pe.wait_ge(oT_out, 1 + t)
                mm(ps[:, 5, 0:P], zeros[:, :], ident[:, :], start=True, stop=False)
                with pe.Fori(0, NP) as j:
                    g = t * NP + j
                    pe.wait_ge(ex_ready, g + 1)
                    for c, s in enumerate((eT_act, eT_dve)):
                        pe.wait_ge(s, 1 + g)
                        for h in range(H):
                            ins = nc.tensor.transpose(ps[:, 3 + c, h * P:(h + 1) * P], e[:, h, c * P:(c + 1) * P], ident[:, :])
                        ins.then_inc(eT_done, 1)
                    pe.wait_ge(vs_ready, g + 1)
                    for c, s in enumerate((eT_act, eT_dve)):
                        pe.wait_ge(s, g + 2)
                        for h in range(H):
                            ins = mm(ps[C * h:C * h + C, 5, 0:P], vs[:, c, C * h:C * h + C], eT[:, c, h, :],
                                     start=False, stop=False, skip_group_check=True)
                    ins.then_inc(pv3_pair, 1)
                mm(ps[:, 5, 0:P], zeros[:, :], ident[:, :], start=False, stop=True).then_inc(pv3_tile, 1)
                pe.wait_ge(oT_out, t + 2)
                pe.wait_ge(o_used, 1 + t)
                nc.tensor.transpose(ps[:, 6, 0:P], outT[:, :], ident[:, :]).then_inc(o_done, 1)


def kernel(**inputs):
    import concourse.bacc as bacc
    from concourse.bass_utils import run_bass_kernel_spmd

    i = {n: np.asarray(v) for n, v in inputs.items()}
    blocks = np.ascontiguousarray(i["adj"].reshape(NB, BW, NQ, MQ, P).transpose(0, 2, 4, 3, 1)).reshape(NB * NQ, P, MQ * BW)
    arrays = {
        "x": i["x"], "adj": i["adj"], "adj_blocks": blocks,
        "k0": i["L0_gnn_kernel"], "b0": i["L0_gnn_bias"], "beta": i["L0_gnn_beta"],
        "hv": i["L1_gnn_H_v"], "w2": np.ascontiguousarray(i["L2_gnn_W"].T), "b2": i["L2_gnn_b"],
        "wq": i["L3_gnn_Wq"], "bq": i["L3_gnn_bq"], "wk": i["L3_gnn_Wk"], "bk": i["L3_gnn_bk"],
        "wv": i["L3_gnn_Wv"], "bv": i["L3_gnn_bv"], "ws": i["L3_gnn_Ws"], "bs": i["L3_gnn_bs"],
        "wb": i["L3_gnn_Wb"],
    }
    nc = bacc.Bacc("TRN2", target_bir_lowering=False, num_devices=1)
    a = {n: nc.dram_tensor("in_" + n, v.shape, mybir.dt.from_np(v.dtype), kind="ExternalInput").ap()
         for n, v in arrays.items()}
    out = nc.dram_tensor("out_x", (N, P), F32, kind="ExternalOutput").ap()
    kv_table = nc.dram_tensor("kv_table", (N, 2 * P), F32, kind="Internal").ap()
    build(nc, a["x"], a["adj"], a["adj_blocks"], a["k0"], a["b0"], a["beta"], a["hv"], a["w2"], a["b2"],
          a["wq"], a["bq"], (a["wk"], a["wv"], a["ws"]), (a["bk"], a["bv"], a["bs"]), a["wb"], out, kv_table)
    r = run_bass_kernel_spmd(nc, [{"in_" + n: np.ascontiguousarray(v) for n, v in arrays.items()}], core_ids=[0])
    return r.results[0]["out_x"]
```

```python
from contextlib import ExitStack

import numpy as np
import concourse.bass as bass
from concourse import mybir

F32 = mybir.dt.float32
BF16 = mybir.dt.bfloat16
I32 = mybir.dt.int32
ALU = mybir.AluOpType
ACT = mybir.ActivationFunctionType
AX = mybir.AxisListType

P = 128
N = 4096
T = N // P
NB = 8
BW = N // NB
TB = BW // P
NQ = 4
MQ = T // NQ
H = 4
C = P // H
PW = 2 * P
NP = N // PW
NC = N // P
ZERO_ROW = NB * P * T * TB
EPS = 1e-5
NEG = -1e30
SCALE = float(np.float32(1.0) / np.float32(np.sqrt(C)))


def build(nc, x, adj, adj_rows, k0, b0, beta, hv, w2, b2, wq, bq, wkvs, bkvs, wb, out, kv_table):
    ctx = ExitStack()
    with ctx:
        def sb(name, shape, dt=F32):
            return ctx.enter_context(nc.sbuf_tensor(name, shape, dt))

        def sem(name):
            return ctx.enter_context(nc.semaphore(name))

        x_sb = sb("x_sb", [P, T, P])
        h_sb = sb("h_sb", [P, T, P])
        stats = sb("stats", [P, T, 6])
        rstd = sb("rstd", [P, T])
        nmean = sb("nmean", [P, T])
        lnw = sb("lnw", [P, 4, T])
        ident = sb("ident", [P, P])
        ones = sb("ones", [P, P])
        zeros = sb("zeros", [P, P])
        k0_sb = sb("k0_sb", [P, P])
        w2_sb = sb("w2_sb", [P, 2, P])
        hv_sb = sb("hv_sb", [P, 1])
        hvb = sb("hvb", [P, P])
        b0_bc = sb("b0_bc", [P, P])
        b2_bc = sb("b2_bc", [P, P])
        beta_sb = sb("beta_sb", [P, T])
        wq_sb = sb("wq_sb", [P, P])
        bq_sb = sb("bq_sb", [P, 1])
        wkvs_sb = sb("wkvs_sb", [P, 3 * P])
        bkvs_bc = sb("bkvs_bc", [P, 3 * P])
        wb_bc = sb("wb_bc", [P, 3 * P])
        hmask = sb("hmask", [P, H])
        h_t = sb("h_t", [P, 2, P])
        hT = sb("hT", [P, 2, P])
        aggT = sb("aggT", [P, BW])
        work = sb("work", [P, 30 * 1024 + 512])

        tri = sb("tri", [P, P], BF16)
        ones_b = sb("ones_b", [P, P], BF16)
        iota_s = sb("iota_s", [P, P, T], BF16)
        iota_c = sb("iota_c", [P, NC, T], BF16)
        iota_m = sb("iota_m", [P, T], BF16)
        iota_p = sb("iota_p", [P, 1])
        gate = sb("gate", [P, TB, T])
        iota_j = sb("iota_j", [P, TB, NP])
        row0 = sb("row0", [P, T])
        seen = sb("seen", [P, TB, T])
        flag = sb("flag", [P, TB, T], BF16)
        pos = sb("pos", [P, TB, T])
        run = sb("run", [P, TB, T])
        stage = sb("stage", [P, 2, 2], I32)
        posi = sb("posi", [P, TB, T], I32)
        sloti = sb("sloti", [P, TB, T], I32)
        slot = sb("slot", [P, TB, T], BF16)
        chunk = sb("chunk", [P, TB, T], BF16)
        more = sb("more", [P, TB, NP])
        pairs = sb("pairs", [P, T])
        ends = sb("ends", [P, T])
        bounds = sb("bounds", [P, T + 1], I32)
        idxf = sb("idxf", [P, 2, NC])
        node_idx = sb("node_idx", [P, T, NC], I32)
        adj_idx = sb("adj_idx", [P, T, NC], I32)

        ring = work[:, 0:4 * 4096].rearrange("p (q m n) -> p q m n", q=NQ, m=MQ)
        selfterm = work[:, 16384:20480].rearrange("p (t f) -> p t f", t=T)
        degp = work[:, 20480:22528].rearrange("p (q n) -> p q n", q=NQ)
        upd = work[:, 22528:23040].rearrange("p (t f) -> p t f", t=TB)
        upd2 = work[:, 23040:23552].rearrange("p (t f) -> p t f", t=TB)
        inv = work[:, 23552:23556]
        rows = work[:, 0:8192].rearrange("p (b m) -> p b m", b=2)
        logit = work[:, 8192:16384].rearrange("p (b m) -> p b m", b=2)
        neg = work[:, 16384:18432].bitcast(BF16)
        score = work[:, 18432:22528]
        probT = work[:, 22528:23552].rearrange("p (b c n) -> p b c n", b=2, c=4)
        mx = work[:, 23552:23554]
        nmx = work[:, 23554:23556]
        den = work[:, 23556:23558]
        rden = work[:, 23558:23560]
        xnew = work[:, 23680:23808]
        onehot = work[:, 23560:27656].bitcast(BF16).rearrange("p (b s m) -> p b s m", b=2, s=P)
        coded = work[:, 27656:30728].bitcast(BF16).rearrange("p (b v c m) -> p b v c m", b=2, v=3, c=NC)
        S = work[:, 0:16384].rearrange("p (j h m) -> p j h m", j=NP, h=H)
        vstore = work[:, 16384:20480].rearrange("p (j c f) -> p j c f", j=NP, c=2)
        qT = work[:, 20480:24576]
        kvg = work[:, 24576:25088].rearrange("p (c f) -> p c f", c=2)
        ag = work[:, 25088:25344].rearrange("p (c n) -> p c n", c=2)
        mneg = work[:, 25344:25600]
        kT = work[:, 25600:25856]
        qz = work[:, 25856:26368].rearrange("p (h n) -> p h n", h=H)
        e = work[:, 26368:27392].rearrange("p (h m) -> p h m", h=H)
        eT = work[:, 27392:28416].rearrange("p (c h n) -> p c h n", c=2, h=H)
        vs = work[:, 28416:28672].rearrange("p (c f) -> p c f", c=2)
        kvrow = work[:, 28672:29184].rearrange("p (b f) -> p b f", b=2)
        outT = work[:, 29184:29312]
        o = work[:, 29312:29440]
        dif = work[:, 29440:29568]
        junk = work[:, 29568:29696]
        fin = work[:, 29696:29824]
        sm = work[:, 29824:29952]
        xr = h_sb

        ps = ctx.enter_context(nc.psum_tensor("ps", [P, 8, 512], F32))

        ld = sem("ld")
        iotas = sem("iotas")
        seen_done = sem("seen_done")
        flag_ready = sem("flag_ready")
        place_done = sem("place_done")
        place_read = sem("place_read")
        coded_ready = sem("coded_ready")
        list_done = sem("list_done")
        list_read = sem("list_read")
        lists_ready = sem("lists_ready")
        link_i = sem("link_i")
        link_t = sem("link_t")
        link_l = sem("link_l")
        more_done = sem("more_done")
        pads = sem("pads")
        staged = [sem("staged0"), sem("staged1")]
        agT_done = sem("agT_done")
        cst = sem("cst")
        chain = sem("chain")
        block = ctx.enter_context(nc.Block())

        stat_done = [sem(f"stat_done{k}") for k in range(4)]
        ln_ready = [sem(f"ln_ready{k}") for k in range(4)]
        var_ready = [sem(f"var_ready{k}") for k in range(4)]
        std_ready = [sem(f"std_ready{k}") for k in range(4)]
        ht_ready = [sem(f"ht_ready{k}") for k in range(4)]
        ht_copied = [sem(f"ht_copied{k}") for k in range(4)]
        tr_done = [sem(f"tr_done{k}") for k in range(4)]
        hT_ready = [sem(f"hT_ready{k}") for k in range(4)]
        proj_done = [sem(f"proj_done{k}") for k in range(4)]
        post_done = [sem(f"post_done{k}") for k in range(4)]
        slot_full = {k: [sem(f"slot_full{k}_{q}") for q in range(NQ)] for k in (0, 2)}
        slot_used = {k: [sem(f"slot_used{k}_{q}") for q in range(NQ)] for k in (0, 2)}
        slot_summed = [sem(f"slot_summed{q}") for q in range(NQ)]
        agg_done = {k: sem(f"agg_done{k}") for k in (0, 2)}
        agg_out = {k: sem(f"agg_out{k}") for k in (0, 2)}
        up_done = {k: sem(f"up_done{k}") for k in (0, 2)}
        up_used = {k: sem(f"up_used{k}") for k in (0, 2)}
        deg_done = sem("deg_done")
        row_full = [sem("row_full0"), sem("row_full1")]
        prod_ready = sem("prod_ready")
        neg_ready = sem("neg_ready")
        lg_ready = sem("lg_ready")
        e_ready = sem("e_ready")
        pT_done = sem("pT_done")
        pT_out = sem("pT_out")
        pv_grp = sem("pv_grp")
        pv_tile = sem("pv_tile")
        pv_used = sem("pv_used")
        kv_stored = [sem("kv_stored0"), sem("kv_stored1")]
        qz_ready = sem("qz_ready")
        g_full = sem("g_full")
        kT_done = sem("kT_done")
        kT_out = sem("kT_out")
        v_kept = sem("v_kept")
        m_used = sem("m_used")
        s_done = sem("s_done")
        s_out = sem("s_out")
        max_ready = sem("max_ready")
        ex_ready = sem("ex_ready")
        sum_used = sem("sum_used")
        eT_done = sem("eT_done")
        eT_act = sem("eT_act")
        eT_dve = sem("eT_dve")
        vs_ready = sem("vs_ready")
        pv3_pair = sem("pv3_pair")
        pv3_tile = sem("pv3_tile")
        oT_out = sem("oT_out")
        o_done = sem("o_done")
        o_used = sem("o_used")
        z_ready = sem("z_ready")
        ez_ready = sem("ez_ready")
        fin_ready = sem("fin_ready")
        fin_out = sem("fin_out")

        primed = [agg_out[0], agg_out[2], up_used[0], up_used[2], up_done[0], up_done[2], deg_done, kT_done,
                  kT_out, v_kept, m_used, s_done, s_out, eT_done, sum_used, pv3_pair, eT_act, eT_dve, oT_out,
                  o_done, o_used, agT_done, place_read, list_read, list_read, list_done,
                  list_done]

        link_ln = [sem(f"link_ln{k}") for k in range(4)]
        link_x = sem("link_x")
        link_up = {k: sem(f"link_up{k}") for k in (0, 2)}
        link_1 = sem("link_1")
        link_1f = sem("link_1f")
        link_3a = sem("link_3a")
        link_3s = sem("link_3s")
        link_3e = sem("link_3e")
        hvb_ready = sem("hvb_ready")
        NLD = 16

        def wait(eng, s, value):
            if isinstance(value, int) and value <= 0:
                return
            eng.wait_ge(s, value)

        def settle(eng):
            eng.nop(nofuse=True)

        def each_tile(eng, body, n=T):
            body(0, 0)
            body(1, 1)
            with eng.Fori(1, n // 2) as i:
                body(2 * i, 0)
                body(2 * i + 1, 1)

        def tile_pairs(eng, t):
            first = eng.value_load(bounds[0:1, bass.ds(t, 1)], min_val=0, max_val=T * NP - 1)
            end = eng.value_load(bounds[0:1, bass.ds(t + 1, 1)], min_val=1, max_val=T * NP)
            return first, end

        def within(g, first):
            return nc.s_assert_within(g - first, 0, NP - 1,
                                      skip_runtime_bounds_check_because="a tile has at most N neighbours")

        class Link:
            def __init__(self, dve, s, per, turn=0):
                self.dve, self.s, self.per, self.base, self.n = dve, s, per, per * turn, 0

            def __call__(self, ins):
                self.n += 1
                assert self.n <= self.per
                ins.then_inc(self.s, 1)
                self.dve.wait_ge(self.s, self.base + self.n)
                settle(self.dve)

            def end(self):
                assert self.n == self.per, self.n

        @block.sync
        def _(sp):
            sp.dma_start(x_sb[:, :, :], x.rearrange("(t p) f -> p t f", p=P)).then_inc(ld, 16)
            for dst, src in ((k0_sb[:, :], k0), (w2_sb[:, :, :], w2.rearrange("(a f) o -> f a o", a=2)),
                             (hv_sb[:, :], hv), (beta_sb[:, :], beta.rearrange("(t p) -> p t", p=P)),
                             (wq_sb[:, :], wq), (bq_sb[:, :], bq.rearrange("(p a) -> p a", a=1)),
                             (b0_bc[:, :], b0.rearrange("(a f) -> a f", a=1).to_broadcast([P, P])),
                             (b2_bc[:, :], b2.rearrange("(a f) -> a f", a=1).to_broadcast([P, P])),
                             (wb_bc[:, :], wb.rearrange("f a -> a f").to_broadcast([P, 3 * P]))):
                with nc.allow_non_contiguous_dma(reason="small constants"):
                    sp.dma_start(dst, src).then_inc(ld, 16)
            for j, (w, b) in enumerate(zip(wkvs, bkvs)):
                sp.dma_start(wkvs_sb[:, j * P:(j + 1) * P], w).then_inc(ld, 16)
                sp.dma_start(bkvs_bc[:, j * P:(j + 1) * P],
                             b.rearrange("(a f) -> a f", a=1).to_broadcast([P, P])).then_inc(ld, 16)

            def block_rows(nb, q):
                return adj_rows[bass.ds(nb * (P * T * TB), P * T * TB), :].rearrange(
                    "(p m t) n -> p m (t n)", p=P, m=T)[:, q * MQ:(q + 1) * MQ, :]

            def stream(k):
                for q in range(NQ):
                    if k == 2:
                        sp.wait_ge(pv_used, T)
                    sp.dma_start(ring[:, q, :, :], block_rows(0, q)).then_inc(slot_full[k][q], 16)
                with sp.Fori(1, NB) as nb:
                    for q in range(NQ):
                        sp.wait_ge(slot_used[k][q] if q < NQ - 1 else agg_done[k], nb)
                        if k == 0:
                            sp.wait_ge(slot_summed[q], nb)
                        sp.dma_start(ring[:, q, :, :], block_rows(nb, q)).then_inc(slot_full[k][q], 16)

            stream(0)
            sp.wait_ge(up_used[0], 1 + NB)
            for b in range(2):
                sp.dma_start(rows[:, b, :], adj[b * P:(b + 1) * P, :]).then_inc(row_full[b], 16)
            with sp.Fori(1, T // 2) as i:
                for b in range(2):
                    sp.wait_ge(prod_ready, 2 * i + b - 1)
                    sp.wait_ge(neg_ready, 2 * i + b - 1)
                    sp.dma_start(rows[:, b, :], adj[bass.ds((2 * i + b) * P, P), :]).then_inc(row_full[b], 16)
            stream(2)
            sp.dma_start(kv_table[N:N + 1, 0:P], zeros[0:1, :]).then_inc(pads, 16)
            sp.dma_start(kv_table[N:N + 1, P:2 * P], zeros[0:1, :]).then_inc(pads, 16)
            with sp.Fori(0, T // 2) as i:
                for b in range(2):
                    sp.wait_ge(post_done[3], 2 * i + b + 1)
                    sp.dma_start(kv_table[bass.ds((2 * i + b) * P, P), :], kvrow[:, b, :]).then_inc(kv_stored[b], 16)
            def store(t):
                sp.wait_ge(fin_ready, t + 1)
                sp.dma_start(out[bass.ds(t * P, P), :], x_sb[:, t, :]).then_inc(fin_out, 16)

            with sp.Fori(0, T) as t:
                store(t)
            sp.wait_ge(fin_out, 16 * T)

        @block.gpsimd
        def _(pool):
            for s in primed:
                pool.sem_inc(s, 1)
            nc.gpsimd.iota(iota_s[:, :, :], [[1, P], [0, T]], 0, 0, True).then_inc(iotas, 1)
            nc.gpsimd.iota(iota_c[:, :, :], [[1, NC], [0, T]], 0, 0, True).then_inc(iotas, 1)
            nc.gpsimd.iota(iota_m[:, :], [[1, T]], 0, 0, True).then_inc(iotas, 1)
            nc.gpsimd.iota(iota_p[:, :], [[1, 1]], 0, 1, True).then_inc(iotas, 1)
            nc.gpsimd.iota(iota_j[:, :, :], [[0, TB], [PW, NP]], 0, 0, True).then_inc(iotas, 1)
            nc.gpsimd.iota(row0[:, :], [[P * T * TB, NB], [1, TB]], -ZERO_ROW, 0, True).then_inc(iotas, 1)
            nc.gpsimd.memset(ones_b[:, :], 1.0).then_inc(iotas, 1)
            nc.gpsimd.memset(tri[:, :], 1.0).then_inc(iotas, 1)
            nc.gpsimd.memset(gate[:, :, :], 1.0).then_inc(iotas, 1)
            pool.wait_ge(iotas, 9)
            nc.gpsimd.memset(gate[:, :, 0:1], 0.0).then_inc(iotas, 1)
            nc.gpsimd.affine_select(out=tri[:, :], in_=tri[:, :], compare_op=ALU.is_gt, fill=0.0,
                                    base=0, pattern=[[1, P]], channel_multiplier=-1).then_inc(iotas, 1)
            nc.gpsimd.memset(ident[:, :], 0.0).then_inc(cst, 1)
            nc.gpsimd.memset(ones[:, :], 1.0).then_inc(cst, 1)
            nc.gpsimd.memset(zeros[:, :], 0.0).then_inc(cst, 1)
            nc.gpsimd.memset(hmask[:, :], 1.0).then_inc(cst, 1)
            pool.wait_ge(cst, 4)
            nc.gpsimd.affine_select(out=ident[:, :], in_=ident[:, :], compare_op=ALU.not_equal, fill=1.0,
                                    base=0, pattern=[[-1, P]], channel_multiplier=1).then_inc(cst, 1)
            nc.gpsimd.affine_select(out=hmask[:, :], in_=hmask[:, :], compare_op=ALU.is_ge, fill=0.0,
                                    base=0, pattern=[[-C, H]], channel_multiplier=1).then_inc(cst, 1)
            pool.wait_ge(cst, 6)
            nc.gpsimd.affine_select(out=hmask[:, :], in_=hmask[:, :], compare_op=ALU.is_ge, fill=0.0,
                                    base=C - 1, pattern=[[C, H]], channel_multiplier=-1).then_inc(cst, 1)

            pool.wait_ge(post_done[1], T)

            def product(t, b):
                pool.wait_ge(row_full[b], 16 * ((t - b) // 2 + 1) if isinstance(t, int) else 8 * (t - b) + 16)
                wait(pool, pT_done, 8 * (t - 1))
                nc.gpsimd.tensor_tensor(logit[:, b, :], rows[:, b, :], score[:, :], ALU.mult).then_inc(prod_ready, 1)

            each_tile(pool, product)
            pool.wait_ge(pads, 32)
            pool.wait_ge(lists_ready, 1)
            for b in range(2):
                pool.wait_ge(kv_stored[b], 16 * (T // 2))
            with pool.Fori(0, T) as t:
                first, end = tile_pairs(pool, t)
                with pool.Fori(first, end) as g:
                    j = within(g, first)
                    pool.wait_ge(kT_done, 1 + g)
                    pool.wait_ge(agT_done, 1 + g)
                    for c in range(2):
                        nc.gpsimd.tensor_copy(stage[:, c, 0:1], node_idx[:, bass.ds(t, 1), bass.ds(2 * j + c, 1)]
                                              .rearrange("p a c -> p (a c)"))
                        nc.gpsimd.tensor_copy(stage[:, c, 1:2], adj_idx[:, bass.ds(t, 1), bass.ds(2 * j + c, 1)]
                                              .rearrange("p a c -> p (a c)")).then_inc(staged[c], 1)
                        pool.wait_ge(staged[c], g + 1)
                        settle(pool)
                        nc.gpsimd.indirect_dma_start(
                            out=kvg[:, c, :], out_offset=None, in_=kv_table,
                            in_offset=bass.IndirectOffsetOnAxis(ap=stage[:, c, 0:1], axis=0)).then_inc(g_full, 16)
                        nc.gpsimd.indirect_dma_start(
                            out=ag[:, c, :], out_offset=None, in_=adj_rows,
                            in_offset=bass.IndirectOffsetOnAxis(ap=stage[:, c, 1:2], axis=0)).then_inc(g_full, 16)
                    pool.wait_ge(g_full, 64 * g + 64)
                    nc.gpsimd.tensor_copy(vstore[:, bass.ds(j, 1), :, :].rearrange("p a c f -> p (a c) f"),
                                          kvg[:, :, P:2 * P]).then_inc(v_kept, 1)
                    pool.wait_ge(v_kept, g + 2)
                with pool.Fori(first, end) as g:
                    j = within(g, first)
                    pool.wait_ge(pv3_pair, 1 + g)
                    nc.gpsimd.tensor_copy(vs[:, :, :], vstore[:, bass.ds(j, 1), :, :]
                                          .rearrange("p a c f -> p (a c) f")).then_inc(vs_ready, 1)

        @block.scalar
        def _(act):
            def normalise(k):
                act.wait_ge(var_ready[k], 1)
                nc.scalar.activation(lnw[:, 3, :], lnw[:, 2, :], ACT.Sqrt).then_inc(std_ready[k], 1)
                act.wait_ge(ln_ready[k], 1)

                def relu(t, b):
                    wait(act, tr_done[k], t - 1)
                    if k < 3:
                        wait(act, ht_copied[k], t - 1)
                    nc.scalar.activation(h_t[:, b, :], x_sb[:, t, :], ACT.Relu, bias=nmean[:, bass.ds(t, 1)],
                                         scale=rstd[:, bass.ds(t, 1)]).then_inc(ht_ready[k], 1)
                each_tile(act, relu)

            def aggregate(k):
                with act.Fori(0, NB) as nb:
                    act.wait_ge(agg_done[k], nb + 1)
                    act.wait_ge(up_done[k], 1 + nb)
                    nc.scalar.activation(aggT[:, :], ps[:, 0, :], ACT.Copy).then_inc(agg_out[k], 1)

            normalise(0)
            aggregate(0)
            normalise(1)

            def exps(t, b):
                act.wait_ge(lg_ready, t + 1)
                wait(act, pv_used, t - 1)
                nc.scalar.activation(logit[:, b, :], logit[:, b, :], ACT.Exp, bias=nmx[:, b:b + 1],
                                     accum_out=den[:, b:b + 1]).then_inc(e_ready, 1)

            def turn(t, lo, hi):
                for n in range(lo, hi):
                    act.wait_ge(pT_done, 8 * t + n + 1)
                    wait(act, pv_grp, 8 * t + n - 1)
                    nc.scalar.activation(probT[:, n % 2, :, :], ps[:, n % 2, :]
                                         .rearrange("p (c n) -> p c n", c=4), ACT.Copy).then_inc(pT_out, 1)

            def layer1(t, b):
                turn(t, 0, 4)
                exps(t + 1, 1 - b)
                turn(t, 4, 8)

            exps(0, 0)
            layer1(0, 0)
            layer1(1, 1)
            with act.Fori(1, T // 2 - 1) as i:
                layer1(2 * i, 0)
                layer1(2 * i + 1, 1)
            layer1(T - 2, 0)
            turn(T - 1, 0, 8)

            normalise(2)
            aggregate(2)
            normalise(3)

            act.wait_ge(lists_ready, 1)
            with act.Fori(0, T) as t:
                first, end = tile_pairs(act, t)
                with act.Fori(first, end) as g:
                    j = within(g, first)
                    act.wait_ge(kT_done, g + 2)
                    act.wait_ge(s_done, 1 + 2 * g)
                    nc.scalar.activation(kT[:, :], ps[:, 0, 0:PW], ACT.Copy).then_inc(kT_out, 1)
                act.wait_ge(max_ready, t + 1)
                with act.Fori(first, end) as g:
                    j = within(g, first)
                    act.wait_ge(eT_done, 1 + 2 * g)
                    act.wait_ge(sum_used, 1 + g)
                    for h in range(H):
                        ins = nc.scalar.activation(e[:, h, :], S[:, bass.ds(j, 1), h, :].rearrange("p a m -> p (a m)"),
                                                   ACT.Exp, bias=sm[:, 8 + h:9 + h], scale=SCALE,
                                                   accum_out=sm[:, 12 + h:13 + h])
                    ins.then_inc(ex_ready, 1)
                    act.wait_ge(eT_done, 2 * g + 2)
                    act.wait_ge(pv3_pair, 1 + g)
                    nc.scalar.activation(eT[:, 0, :, :], ps[:, 3, :].rearrange("p (h n) -> p h n", h=H),
                                         ACT.Copy).then_inc(eT_act, 1)
                act.wait_ge(pv3_tile, t + 1)
                act.wait_ge(o_done, 1 + t)
                nc.scalar.activation(outT[:, :], ps[:, 5, 0:P], ACT.Copy).then_inc(oT_out, 1)
                act.wait_ge(z_ready, t + 1)
                nc.scalar.activation(sm[:, 41:42], sm[:, 40:41], ACT.Exp, scale=-1.0).then_inc(ez_ready, 1)

        @block.vector
        def _(dve):
            dve.wait_ge(ld, 16 * NLD)
            dve.wait_ge(cst, 7)
            dve.wait_ge(iotas, 11)
            nc.vector.tensor_scalar(hvb[:, :], ones[:, :], hv_sb[:, 0:1], None, ALU.mult).then_inc(hvb_ready, 1)

            def row_stats(k, nb):
                for j in range(TB):
                    ins = nc.vector.bn_stats(stats[:, TB * nb + j, :], x_sb[:, TB * nb + j, :])
                ins.then_inc(stat_done[k], 1)

            def moments(k, count):
                dve.wait_ge(stat_done[k], count)
                link = Link(dve, link_ln[k], 8)
                a, d, v, sd = (lnw[:, n, :] for n in range(4))
                me, mo, ve, vo = (stats[:, :, n] for n in (1, 4, 2, 5))
                link(nc.vector.tensor_tensor(d, me, mo, ALU.subtract))
                link(nc.vector.tensor_tensor(a, ve, vo, ALU.add))
                link(nc.vector.tensor_tensor(d, d, d, ALU.mult))
                link(nc.vector.tensor_scalar(a, a, 1.0 / P, EPS, ALU.mult, ALU.add))
                link(nc.vector.scalar_tensor_tensor(v, d, 0.25, a, ALU.mult, ALU.add))
                nc.vector.tensor_tensor(a, me, mo, ALU.add).then_inc(var_ready[k], 1)
                dve.wait_ge(var_ready[k], 1)
                dve.wait_ge(std_ready[k], 1)
                link(nc.vector.reciprocal(rstd[:, :], sd))
                link(nc.vector.scalar_tensor_tensor(nmean[:, :], a, -0.5, rstd[:, :], ALU.mult, ALU.mult))
                link(nc.vector.tensor_copy(lnw[:, 1, :], rstd[:, :]))
                link.end()
                nc.vector.tensor_copy(lnw[:, 0, :], nmean[:, :]).then_inc(ln_ready[k], 1)

            def node_terms(k):
                def tile(t, b):
                    dve.wait_ge(ht_ready[k], t + 1)
                    if k < 3:
                        nc.vector.tensor_copy(h_sb[:, t, :], h_t[:, b, :]).then_inc(ht_copied[k], 1)
                    dve.wait_ge(tr_done[k], t + 1)
                    wait(dve, proj_done[k], t - 1)
                    nc.vector.tensor_copy(hT[:, b, :], ps[:, b, 0:P]).then_inc(hT_ready[k], 1)
                    dve.wait_ge(proj_done[k], t + 1)
                    got = ps[:, 2 + b, 0:P]
                    if k == 0:
                        ins = nc.vector.tensor_scalar(selfterm[:, t, :], got, beta_sb[:, bass.ds(t, 1)], None, ALU.mult)
                    elif k == 1:
                        ins = nc.vector.tensor_copy(score[:, bass.ds(t * P, P)], got)
                    elif k == 2:
                        ins = nc.vector.tensor_tensor(selfterm[:, t, :], got, b2_bc[:, :], ALU.add)
                    else:
                        if not isinstance(t, int):
                            dve.wait_ge(kv_stored[b], 8 * (t - b))
                        nc.vector.tensor_tensor(kvrow[:, b, :], ps[:, 2 + b, 0:2 * P], bkvs_bc[:, 0:2 * P], ALU.add)
                        nc.vector.tensor_tensor(xr[:, t, :], ps[:, 2 + b, 2 * P:3 * P], bkvs_bc[:, 2 * P:3 * P], ALU.add)
                        ins = nc.vector.tensor_scalar(qT[:, bass.ds(t * P, P)], ps[:, 4 + b, 0:P], bq_sb[:, 0:1],
                                                      None, ALU.add)
                    ins.then_inc(post_done[k], 1)
                each_tile(dve, tile)

            def place(nb):
                link = Link(dve, link_i, 9, nb)
                nc.vector.tensor_scalar(flag[:, :, :], seen[:, :, :], 0.0, None, ALU.not_equal).then_inc(flag_ready, 1)
                dve.wait_ge(place_done, nb + 1)
                before, of_tile = (ps[:, 6, 128 * n + 128:128 * n + 256] for n in range(2))
                flat = (lambda a: a[:, :, :].rearrange("p t m -> p (t m)"))
                link(nc.vector.tensor_tensor_scan(flat(run), flat(gate), of_tile, 0.0, ALU.mult, ALU.add))
                link(nc.vector.tensor_tensor(flat(pos), flat(run), of_tile, ALU.subtract))
                nc.vector.tensor_tensor(flat(pos), flat(pos), before, ALU.add).then_inc(place_read, 1)
                dve.wait_ge(place_read, nb + 2)
                link(nc.vector.scalar_tensor_tensor(flat(pos), flat(flag), -2.0 * N, flat(pos), ALU.mult, ALU.add))
                link(nc.vector.tensor_scalar(flat(posi), flat(pos), 2.0 * N, None, ALU.add))
                link(nc.vector.tensor_scalar(flat(sloti), flat(posi), P - 1, None, ALU.bitwise_and))
                link(nc.vector.tensor_copy(flat(slot), flat(sloti)))
                link(nc.vector.tensor_scalar(flat(sloti), flat(posi), 7, None, ALU.logical_shift_right))
                link(nc.vector.tensor_copy(flat(chunk), flat(sloti)))
                link(nc.vector.tensor_tensor(more[:, :, :], run[:, :, T - 1:T].to_broadcast([P, TB, NP]),
                                             iota_j[:, :, :], ALU.is_gt))
                nc.vector.tensor_reduce(ends[:, 0:TB], more[:, :, :], AX.X, ALU.add).then_inc(more_done, 1)
                dve.wait_ge(more_done, 2 * nb + 1)
                nc.vector.tensor_scalar(pairs[:, bass.ds(nb * TB, TB)], ends[:, 0:TB], 1.0, None,
                                        ALU.max).then_inc(more_done, 1)
                link.end()

            def code(nb, j):
                b = j % 2
                n = nb * TB + j
                dve.wait_ge(list_done, n + 1)
                nc.vector.tensor_tensor(onehot[:, b, :, :], iota_s[:, :, :], slot[:, j:j + 1, :]
                                        .to_broadcast([P, P, T]), ALU.is_equal)
                nc.vector.tensor_tensor(coded[:, b, 2, :, :], iota_c[:, :, :], chunk[:, j:j + 1, :]
                                        .to_broadcast([P, NC, T]), ALU.is_equal).then_inc(link_t, 1)
                dve.wait_ge(link_t, n + 1)
                nc.vector.tensor_tensor(coded[:, b, 0, :, :], coded[:, b, 2, :, :], iota_m[:, :]
                                        .rearrange("p (a m) -> p a m", a=1).to_broadcast([P, NC, T]), ALU.mult)
                nc.vector.tensor_scalar(coded[:, b, 1, :, :], coded[:, b, 2, :, :], iota_p[:, 0:1], None,
                                        ALU.mult).then_inc(coded_ready, 1)

            def lists(nb, j):
                n = nb * TB + j
                link = Link(dve, link_l, 4, n)
                dve.wait_ge(list_read, n + 2)
                dve.wait_ge(list_done, n + 3)
                got = ps[:, 7 if j % 2 else 3, 0:3 * NC].rearrange("p (v c) -> p v c", v=3)
                link(nc.vector.tensor_scalar(idxf[:, 0, :], got[:, 2, :], -float(N), float(N), ALU.mult, ALU.add))
                link(nc.vector.scalar_tensor_tensor(idxf[:, 0, :], got[:, 0, :], float(P), idxf[:, 0, :], ALU.mult, ALU.add))
                link(nc.vector.tensor_scalar(idxf[:, 1, :], got[:, 2, :], row0[:, bass.ds(n, 1)], float(ZERO_ROW),
                                             ALU.mult, ALU.add))
                link(nc.vector.scalar_tensor_tensor(idxf[:, 1, :], got[:, 0, :], float(TB), idxf[:, 1, :], ALU.mult, ALU.add))
                nc.vector.tensor_tensor(node_idx[:, n, :], idxf[:, 0, :], got[:, 1, :], ALU.add)
                nc.vector.scalar_tensor_tensor(adj_idx[:, n, :], got[:, 1, :], float(T * TB), idxf[:, 1, :], ALU.mult,
                                               ALU.add).then_inc(list_read, 1)
                link.end()

            def find_neighbours(nb):
                place(nb)
                code(nb, 0)
                code(nb, 1)
                for j in range(TB):
                    lists(nb, j)
                    if j + 2 < TB:
                        code(nb, j + 2)

            def number_pairs():
                dve.wait_ge(more_done, 2 * NB)
                nc.vector.memset(bounds[:, 0:1], 0.0)
                nc.vector.tensor_tensor_scan(ends[:, :], ones[:, 0:T], pairs[:, :], 0.0, ALU.mult, ALU.add).then_inc(more_done, 1)
                dve.wait_ge(more_done, 2 * NB + 1)
                nc.vector.tensor_copy(bounds[:, 1:T + 1], ends[:, :]).then_inc(lists_ready, 1)

            def update(k):
                with dve.Fori(0, NB) as nb:
                    link = Link(dve, link_up[k], 5 if k == 0 else 2, nb)
                    xs = x_sb[:, bass.ds(nb * TB, TB), :]
                    own = selfterm[:, bass.ds(nb * TB, TB), :]
                    got = ps[:, 1, :].rearrange("p (t f) -> p t f", t=TB)
                    if k == 0:
                        for q in range(NQ):
                            dve.wait_ge(slot_full[k][q], 16 * nb + 16)
                            if q == 0:
                                dve.wait_ge(deg_done, 1 + nb)
                            nc.vector.tensor_reduce(degp[:, q, :], ring[:, q, :, :].rearrange("p m n -> p n m"),
                                                    AX.X, ALU.add)
                            nc.vector.tensor_reduce(
                                seen[:, :, q * MQ:(q + 1) * MQ].rearrange("p t m -> p m t"),
                                ring[:, q, :, :].rearrange("p m (t n) -> p m t n", t=TB), AX.X, ALU.max,
                                apply_absolute_value=True).then_inc(slot_summed[q], 1)
                        for q in range(NQ):
                            dve.wait_ge(slot_summed[q], nb + 1)
                        find_neighbours(nb)
                        dve.wait_ge(deg_done, nb + 2)
                        link(nc.vector.tensor_tensor(inv, ps[:, 6, 0:TB], beta_sb[:, bass.ds(nb * TB, TB)], ALU.add))
                        link(nc.vector.reciprocal(inv, inv))
                        dve.wait_ge(up_done[k], nb + 2)
                        nc.vector.tensor_tensor(upd, got, own, ALU.add).then_inc(up_used[k], 1)
                        dve.wait_ge(up_used[k], nb + 2)
                        link(nc.vector.tensor_tensor(upd2, upd, inv.rearrange("p (t a) -> p t a", a=1)
                                                     .to_broadcast([P, TB, P]), ALU.mult))
                        link(nc.vector.tensor_tensor(upd, upd2, b0_bc[:, :].rearrange("p (a f) -> p a f", a=1)
                                                     .to_broadcast([P, TB, P]), ALU.add))
                        link(nc.vector.tensor_tensor(xs, upd, xs, ALU.add))
                    else:
                        dve.wait_ge(up_done[k], nb + 2)
                        nc.vector.tensor_tensor(upd, got, own, ALU.add).then_inc(up_used[k], 1)
                        dve.wait_ge(up_used[k], nb + 2)
                        link(nc.vector.tensor_scalar(upd2, upd, 0.0, None, ALU.max))
                        link(nc.vector.tensor_tensor(xs, upd2, xs, ALU.add))
                    link.end()
                    row_stats(k + 1, nb)

            with dve.Fori(0, NB) as nb:
                row_stats(0, nb)
            moments(0, NB)
            node_terms(0)
            update(0)
            number_pairs()
            moments(1, NB)
            node_terms(1)

            def mask_and_max(t, b):
                dve.wait_ge(row_full[b], 16 * (t // 2) + 16 if isinstance(t, int) else 8 * (t - b) + 16)
                nc.vector.tensor_scalar(neg, rows[:, b, :], 0.0, NEG, ALU.is_equal, ALU.mult).then_inc(neg_ready, 1)
                dve.wait_ge(neg_ready, t + 1)
                dve.wait_ge(prod_ready, t + 1)
                wait(dve, e_ready, t - 1)
                settle(dve)
                link = Link(dve, link_1, 1, t)
                link(nc.vector.tensor_tensor_reduce(out=logit[:, b, :], in0=logit[:, b, :], in1=neg, scale=1.0,
                                                    scalar=-3.0e38, op0=ALU.add, op1=ALU.max,
                                                    accum_out=mx[:, b:b + 1]))
                link.end()
                nc.vector.tensor_scalar(nmx[:, b:b + 1], mx[:, b:b + 1], -1.0, None, ALU.mult).then_inc(lg_ready, 1)

            def mean_and_add(t, b):
                link = Link(dve, link_1f, 2, t)
                dve.wait_ge(e_ready, t + 1)
                link(nc.vector.reciprocal(rden[:, b:b + 1], den[:, b:b + 1]))
                dve.wait_ge(pv_grp, 8 * t + 8)
                link(nc.vector.scalar_tensor_tensor(xnew, ps[:, 4 + b, 0:P], rden[:, b:b + 1],
                                                    x_sb[:, t, :], ALU.mult, ALU.add))
                link.end()
                nc.vector.tensor_copy(x_sb[:, t, :], xnew).then_inc(pv_used, 1)
                nc.vector.bn_stats(stats[:, t, :], xnew).then_inc(stat_done[2], 1)

            mask_and_max(0, 0)
            mask_and_max(1, 1)
            mean_and_add(0, 0)
            with dve.Fori(1, T // 2) as i:
                mask_and_max(2 * i, 0)
                mean_and_add(2 * i - 1, 1)
                mask_and_max(2 * i + 1, 1)
                mean_and_add(2 * i, 0)
            mean_and_add(T - 1, 1)
            moments(2, T)
            node_terms(2)
            update(2)
            moments(3, NB)
            node_terms(3)

            pmax, rmax, nmax, part, total = (sm[:, 4 * n:4 * n + 4] for n in range(5))
            some, rl = sm[:, 20:24], sm[:, 24:28]
            z = [sm[:, 38:39], sm[:, 39:40], sm[:, 40:41]]
            ez, nb_ = sm[:, 41:42], sm[:, 42:43]
            dve.wait_ge(lists_ready, 1)
            with dve.Fori(0, T) as t:
                first, end = tile_pairs(dve, t)
                link = Link(dve, link_3s, 14, t)
                nc.vector.memset(rmax, -3.0e38)
                nc.vector.memset(total, 0.0)
                nc.vector.tensor_tensor(qz[:, :, :], qT[:, bass.ds(t * P, P)].rearrange("p (a n) -> p a n", a=1)
                                        .to_broadcast([P, H, P]), hmask[:, :].rearrange("p (h a) -> p h a", a=1)
                                        .to_broadcast([P, H, P]), ALU.mult).then_inc(qz_ready, 1)
                dve.wait_ge(qz_ready, t + 1)
                settle(dve)
                with dve.Fori(first, end) as g:
                    j = within(g, first)
                    step = Link(dve, link_3a, 2, g)
                    dve.wait_ge(agT_done, g + 2)
                    nc.vector.tensor_scalar(mneg[:, :], ps[:, 7, 0:PW], 0.0, NEG, ALU.is_equal, ALU.mult).then_inc(m_used, 1)
                    dve.wait_ge(m_used, g + 2)
                    for f in range(2):
                        dve.wait_ge(s_done, 2 * g + f + 2)
                        nc.vector.tensor_tensor(S[:, bass.ds(j, 1), 2 * f:2 * f + 2, :].rearrange("p a h m -> p (a h) m"),
                                                ps[:, 1 + f, :].rearrange("p (h m) -> p h m", h=2),
                                                mneg[:, :].rearrange("p (a m) -> p a m", a=1).to_broadcast([P, 2, PW]),
                                                ALU.add).then_inc(s_out, 1)
                    dve.wait_ge(s_out, 1 + 2 * g + 2)
                    settle(dve)
                    step(nc.vector.tensor_reduce(pmax, S[:, bass.ds(j, 1), :, :].rearrange("p a h m -> p (a h) m"),
                                                 AX.X, ALU.max))
                    step(nc.vector.tensor_tensor(rmax, rmax, pmax, ALU.max))
                    step.end()
                nc.vector.tensor_scalar(nmax, rmax, -SCALE, None, ALU.mult).then_inc(max_ready, 1)
                link(nc.vector.tensor_scalar(some, rmax, 0.5 * NEG, None, ALU.is_gt))
                with dve.Fori(first, end) as g:
                    j = within(g, first)
                    dve.wait_ge(ex_ready, g + 1)
                    nc.vector.tensor_tensor(total, total, part, ALU.add).then_inc(sum_used, 1)
                    dve.wait_ge(eT_done, 1 + 2 * g + 2)
                    dve.wait_ge(pv3_pair, 1 + g)
                    nc.vector.tensor_copy(eT[:, 1, :, :], ps[:, 4, :].rearrange("p (h n) -> p h n", h=H)).then_inc(eT_dve, 1)
                dve.wait_ge(sum_used, 1 + end)
                link(nc.vector.reciprocal(rl, total))
                link(nc.vector.tensor_tensor(rl, rl, some, ALU.mult))
                link(nc.vector.tensor_copy(fin[:, :], xr[:, t, :]))
                dve.wait_ge(o_done, t + 2)
                nc.vector.tensor_tensor(o[:, :].rearrange("p (c h) -> p h c", h=H),
                                        ps[:, 6, 0:P].rearrange("p (h c) -> p h c", h=H),
                                        rl.rearrange("p (h a) -> p h a", a=1).to_broadcast([P, H, C]),
                                        ALU.mult).then_inc(o_used, 1)
                dve.wait_ge(o_used, t + 2)
                link(nc.vector.tensor_tensor(dif[:, :], o[:, :], fin[:, :], ALU.subtract))
                for n, v in enumerate((o, fin, dif)):
                    ins = nc.vector.tensor_tensor_reduce(out=junk[:, :], in0=v[:, :], in1=wb_bc[:, n * P:(n + 1) * P],
                                                         scale=1.0, scalar=z[n - 1] if n else 0.0, op0=ALU.mult,
                                                         op1=ALU.add, accum_out=z[n])
                    if n < 2:
                        link(ins)
                ins.then_inc(z_ready, 1)
                dve.wait_ge(ez_ready, t + 1)
                link(nc.vector.tensor_scalar(ez, ez, -1.0, -1.0, ALU.mult, ALU.add))
                link(nc.vector.reciprocal(nb_, ez))
                link(nc.vector.scalar_tensor_tensor(junk[:, :], dif[:, :], nb_, o[:, :], ALU.mult, ALU.add))
                link(nc.vector.tensor_copy(fin[:, :], x_sb[:, t, :]))
                link(nc.vector.tensor_tensor(fin[:, :], fin[:, :], junk[:, :], ALU.add))
                link(nc.vector.tensor_copy(x_sb[:, t, :], fin[:, :]))
                link(nc.vector.memset(junk[:, 0:1], 0.0))
                link.end()
                nc.vector.memset(junk[:, 0:1], 0.0).then_inc(fin_ready, 1)

        @block.tensor
        def _(pe):
            mm = nc.tensor.matmul
            pe.wait_ge(cst, 7)
            pe.wait_ge(iotas, 11)
            pe.wait_ge(ld, 16 * NLD)
            pe.wait_ge(hvb_ready, 1)

            def project(k):
                def tile(t, b):
                    pe.wait_ge(ht_ready[k], t + 1)
                    wait(pe, hT_ready[k], t - 1)
                    nc.tensor.transpose(ps[:, b, 0:P], h_t[:, b, :], ident[:, :]).then_inc(tr_done[k], 1)
                    pe.wait_ge(hT_ready[k], t + 1)
                    wait(pe, post_done[k], t - 1)
                    got = ps[:, 2 + b, 0:P]
                    if k == 0:
                        ins = mm(got, hT[:, b, :], k0_sb[:, :], start=True, stop=True)
                    elif k == 1:
                        ins = mm(got, hvb[:, :], hT[:, b, :], start=True, stop=True)
                    elif k == 2:
                        ins = mm(got, hT[:, b, :], w2_sb[:, 0, :], start=True, stop=True)
                    else:
                        mm(ps[:, 2 + b, 0:3 * P], hT[:, b, :], wkvs_sb[:, :], start=True, stop=True)
                        ins = mm(ps[:, 4 + b, 0:P], wq_sb[:, :], hT[:, b, :], start=True, stop=True)
                    ins.then_inc(proj_done[k], 1)
                each_tile(pe, tile)

            def find_neighbours(nb):
                pe.wait_ge(flag_ready, nb + 1)
                pe.wait_ge(place_read, nb + 1)
                flags = flag[:, :, :].rearrange("p t m -> p (t m)")
                mm(ps[:, 6, 128:256], tri[:, :], flags, start=True, stop=True)
                mm(ps[:, 6, 256:384], ones_b[:, :], flags, start=True, stop=True).then_inc(place_done, 1)
                for j in range(TB):
                    n = nb * TB + j
                    pe.wait_ge(coded_ready, n + 1)
                    pe.wait_ge(list_read, n + 1)
                    for m in range(T):
                        ins = mm(ps[:, 7 if j % 2 else 3, 0:3 * NC], onehot[:, j % 2, :, m],
                                 coded[:, j % 2, :, :, m].rearrange("p v c -> p (v c)"), start=(m == 0), stop=(m == T - 1))
                    ins.then_inc(list_done, 1)

            def aggregate(k):
                pe.wait_ge(ht_copied[k], T)
                pe.wait_ge(post_done[k], T)
                with pe.Fori(0, NB) as nb:
                    pe.wait_ge(agg_out[k], 1 + nb)
                    for q in range(NQ):
                        pe.wait_ge(slot_full[k][q], 16 * nb + 16)
                        for m in range(MQ):
                            ins = mm(ps[:, 0, :], h_sb[:, q * MQ + m, :], ring[:, q, m, :],
                                     start=(q + m == 0), stop=(q * MQ + m == T - 1))
                        if q < NQ - 1:
                            ins.then_inc(slot_used[k][q], 1)
                    ins.then_inc(agg_done[k], 1)
                    pe.wait_ge(up_used[k], 1 + nb)
                    if k == 0:
                        find_neighbours(nb)
                    if k == 0:
                        for q in range(NQ):
                            pe.wait_ge(slot_summed[q], nb + 1)
                        for j in range(TB):
                            for q in range(NQ):
                                ins = mm(ps[:, 6, j:j + 1], degp[:, q, j * P:(j + 1) * P], ones[:, 0:1],
                                         start=(q == 0), stop=(q == NQ - 1))
                        ins.then_inc(deg_done, 1)
                    pe.wait_ge(agg_out[k], nb + 2)
                    for j in range(TB):
                        ins = mm(ps[:, 1, j * P:(j + 1) * P], aggT[:, j * P:(j + 1) * P],
                                 k0_sb[:, :] if k == 0 else w2_sb[:, 1, :], start=True, stop=True)
                    ins.then_inc(up_done[k], 1)

            project(0)
            aggregate(0)
            project(1)

            def transposes(t, b, n):
                if n == 0:
                    pe.wait_ge(e_ready, t + 1)
                wait(pe, pT_out, 8 * t + n - 1)
                for c in range(4):
                    m = 4 * n + c
                    ins = nc.tensor.transpose(ps[:, n % 2, c * P:(c + 1) * P], logit[:, b, m * P:(m + 1) * P], ident[:, :])
                ins.then_inc(pT_done, 1)

            def weighted(t, b, n):
                if n == 0:
                    wait(pe, pv_used, t - 1)
                pe.wait_ge(pT_out, 8 * t + n + 1)
                for c in range(4):
                    m = 4 * n + c
                    ins = mm(ps[:, 4 + b, 0:P], probT[:, n % 2, c, :], h_sb[:, m, :], start=(m == 0), stop=(m == T - 1))
                ins.then_inc(pv_grp, 1)

            def layer1(t, b):
                transposes(t, b, 0)
                for n in range(8):
                    if n < 7:
                        transposes(t, b, n + 1)
                    weighted(t, b, n)

            pe.wait_ge(ht_copied[1], T)
            pe.wait_ge(post_done[1], T)
            each_tile(pe, layer1)

            project(2)
            aggregate(2)
            project(3)

            pe.wait_ge(lists_ready, 1)
            with pe.Fori(0, T) as t:
                first, end = tile_pairs(pe, t)
                pe.wait_ge(qz_ready, t + 1)
                settle(pe)
                with pe.Fori(first, end) as g:
                    j = within(g, first)
                    pe.wait_ge(g_full, 64 * g + 64)
                    pe.wait_ge(kT_out, 1 + g)
                    for c in range(2):
                        ins = nc.tensor.transpose(ps[:, 0, c * P:(c + 1) * P], kvg[:, c, 0:P], ident[:, :])
                    ins.then_inc(kT_done, 1)
                    pe.wait_ge(m_used, 1 + g)
                    for c in range(2):
                        ins = nc.tensor.transpose(ps[:, 7, c * P:(c + 1) * P], ag[:, c, :], ident[:, :])
                    ins.then_inc(agT_done, 1)
                    pe.wait_ge(kT_out, g + 2)
                    pe.wait_ge(s_out, 1 + 2 * g)
                    for f in range(2):
                        for u in range(2):
                            ins = mm(ps[:, 1 + f, u * PW:(u + 1) * PW], qz[:, 2 * f + u, :], kT[:, :], start=True, stop=True)
                        ins.then_inc(s_done, 1)
                pe.wait_ge(oT_out, 1 + t)
                mm(ps[:, 5, 0:P], zeros[:, :], ident[:, :], start=True, stop=False)
                with pe.Fori(first, end) as g:
                    j = within(g, first)
                    pe.wait_ge(ex_ready, g + 1)
                    for c, s in enumerate((eT_act, eT_dve)):
                        pe.wait_ge(s, 1 + g)
                        for h in range(H):
                            ins = nc.tensor.transpose(ps[:, 3 + c, h * P:(h + 1) * P], e[:, h, c * P:(c + 1) * P], ident[:, :])
                        ins.then_inc(eT_done, 1)
                    pe.wait_ge(vs_ready, g + 1)
                    for c, s in enumerate((eT_act, eT_dve)):
                        pe.wait_ge(s, g + 2)
                        for h in range(H):
                            ins = mm(ps[C * h:C * h + C, 5, 0:P], vs[:, c, C * h:C * h + C], eT[:, c, h, :],
                                     start=False, stop=False, skip_group_check=True)
                    ins.then_inc(pv3_pair, 1)
                mm(ps[:, 5, 0:P], zeros[:, :], ident[:, :], start=False, stop=True).then_inc(pv3_tile, 1)
                pe.wait_ge(oT_out, t + 2)
                pe.wait_ge(o_used, 1 + t)
                nc.tensor.transpose(ps[:, 6, 0:P], outT[:, :], ident[:, :]).then_inc(o_done, 1)


def kernel(**inputs):
    import concourse.bacc as bacc
    from concourse.bass_utils import run_bass_kernel_spmd

    i = {n: np.asarray(v) for n, v in inputs.items()}
    blocks = i["adj"].reshape(NB, TB, P, T, P).transpose(0, 4, 3, 1, 2).reshape(ZERO_ROW, P)
    blocks = np.concatenate([blocks, np.zeros((P, P), blocks.dtype)])
    arrays = {
        "x": i["x"], "adj": i["adj"], "adj_rows": blocks,
        "k0": i["L0_gnn_kernel"], "b0": i["L0_gnn_bias"], "beta": i["L0_gnn_beta"],
        "hv": i["L1_gnn_H_v"], "w2": np.ascontiguousarray(i["L2_gnn_W"].T), "b2": i["L2_gnn_b"],
        "wq": i["L3_gnn_Wq"], "bq": i["L3_gnn_bq"], "wk": i["L3_gnn_Wk"], "bk": i["L3_gnn_bk"],
        "wv": i["L3_gnn_Wv"], "bv": i["L3_gnn_bv"], "ws": i["L3_gnn_Ws"], "bs": i["L3_gnn_bs"],
        "wb": i["L3_gnn_Wb"],
    }
    nc = bacc.Bacc("TRN2", target_bir_lowering=False, num_devices=1)
    a = {n: nc.dram_tensor("in_" + n, v.shape, mybir.dt.from_np(v.dtype), kind="ExternalInput").ap()
         for n, v in arrays.items()}
    out = nc.dram_tensor("out_x", (N, P), F32, kind="ExternalOutput").ap()
    kv_table = nc.dram_tensor("kv_table", (N + 1, 2 * P), F32, kind="Internal").ap()
    build(nc, a["x"], a["adj"], a["adj_rows"], a["k0"], a["b0"], a["beta"], a["hv"], a["w2"], a["b2"],
          a["wq"], a["bq"], (a["wk"], a["wv"], a["ws"]), (a["bk"], a["bv"], a["bs"]), a["wb"], out, kv_table)
    r = run_bass_kernel_spmd(nc, [{"in_" + n: np.ascontiguousarray(v) for n, v in arrays.items()}], core_ids=[0])
    return r.results[0]["out_x"]
```

```python
from contextlib import ExitStack

import numpy as np
import concourse.bass as bass
from concourse import mybir

F32 = mybir.dt.float32
BF16 = mybir.dt.bfloat16
I32 = mybir.dt.int32
ALU = mybir.AluOpType
ACT = mybir.ActivationFunctionType
AX = mybir.AxisListType

P = 128
N = 4096
T = N // P
NB = 8
BW = N // NB
TB = BW // P
NQ = 4
MQ = T // NQ
SEEN = 2 * (NQ - 1)
H = 4
C = P // H
NC = N // P
QC = 4
QW = QC * P
HALF = QC // 2
NP = N // QW
QUADS = T * NP
NBUF = 3
STEPS = -(-QUADS // NBUF)
BEHIND = NBUF + 1
ZERO_ROW = NB * P * T * TB
FT = 8
EPS = 1e-5
NEG = -1e30
HIGH = 1e30
LOW = 0.1 * NEG
TINY = 1e-30
SCALE = float(np.float32(1.0) / np.float32(np.sqrt(C)))


def build(nc, x, adj_rows, k0, b0, beta, hv, w2, b2, wq, bq, wkvs, bkvs, wb, out, h1_table, h2_table, kv_table,
          adj_table):
    ctx = ExitStack()
    with ctx:
        def sb(name, shape, dt=F32):
            return ctx.enter_context(nc.sbuf_tensor(name, shape, dt))

        def sem(name):
            return ctx.enter_context(nc.semaphore(name))

        x_sb = sb("x_sb", [P, T, P])
        h_sb = sb("h_sb", [P, T, P])
        stats = sb("stats", [P, T, 6])
        rstd = sb("rstd", [P, T])
        nmean = sb("nmean", [P, T])
        lnw = sb("lnw", [P, 4, T])
        ident = sb("ident", [P, P])
        ones = sb("ones", [P, P])
        zeros = sb("zeros", [P, P])
        k0_sb = sb("k0_sb", [P, P])
        w2_sb = sb("w2_sb", [P, 2, P])
        b0_bc = sb("b0_bc", [P, P])
        b2_bc = sb("b2_bc", [P, P])
        beta_sb = sb("beta_sb", [P, T])
        wq_sb = sb("wq_sb", [P, P])
        bq_sb = sb("bq_sb", [P, 1])
        wkvs_sb = sb("wkvs_sb", [P, 3 * P])
        bkvs_bc = sb("bkvs_bc", [P, 3 * P])
        wb_bc = sb("wb_bc", [P, 3 * P])
        hv_bc = sb("hv_bc", [P, P])
        hmask = sb("hmask", [P, H])
        h_t = sb("h_t", [P, 2, P + 1])
        hT = sb("hT", [P, 2, P])
        aggT = sb("aggT", [P, BW])
        totals = {k: sb(f"totals{k}", [P, T + 1, n]) for k, n in ((1, 1), (3, H))}
        tops = {k: sb(f"tops{k}", [P, T + 1, n]) for k, n in ((1, 1), (3, H))}
        rden = sb("rden", [P, FT, H])
        some = sb("some", [P, FT, H])
        zed = sb("zed", [P, FT, 1])
        unread = sb("unread", [P, MQ // 2 * TB, P], BF16)
        tiny = sb("tiny", [P, 1])
        work = sb("work", [P, 31240])

        tri = sb("tri", [P, P], BF16)
        ones_b = sb("ones_b", [P, P], BF16)
        iota_s = sb("iota_s", [P, P, T], BF16)
        iota_c = sb("iota_c", [P, NC, T], BF16)
        iota_m = sb("iota_m", [P, T], BF16)
        iota_p = sb("iota_p", [P, 1])
        gate = sb("gate", [P, TB, T])
        iota_j = sb("iota_j", [P, TB, NP])
        row0 = sb("row0", [P, T])
        seen = sb("seen", [P, 2, TB, T])
        flag = sb("flag", [P, TB, T], BF16)
        pos = sb("pos", [P, TB, T])
        run = sb("run", [P, TB, T])
        stage = sb("stage", [P, NBUF, QC], I32)
        posi = sb("posi", [P, TB, T], I32)
        sloti = sb("sloti", [P, TB, T], I32)
        slot = sb("slot", [P, TB, T], BF16)
        chunk = sb("chunk", [P, TB, T], BF16)
        more = sb("more", [P, TB, NP])
        ends4 = sb("ends4", [P, TB])
        last_end = sb("last_end", [P, 1])
        quads = sb("quads", [P, TB])
        ends = sb("ends", [P, T + 1])
        bounds = sb("bounds", [P, T + 1], I32)
        step_at = sb("step_at", [P, STEPS])
        steps = sb("steps", [P, 1])
        stepsi = sb("stepsi", [P, 1], I32)
        qnum = sb("qnum", [P, 3])
        qcmp = sb("qcmp", [P, 3, T])
        qval = sb("qval", [P, 3, 3])
        qdiag = sb("qdiag", [P, 3, P])
        quad_col = sb("quad_col", [P, 3 * P], I32)
        quad_tile = sb("quad_tile", [P, 3 * P], I32)
        quad_first = sb("quad_first", [P, 3 * P])
        cap = sb("cap", [P, 3 * P])
        idxf = sb("idxf", [P, 2, NC])
        node_idx = sb("node_idx", [P, T + 1, NC], I32)
        adj_idx = sb("adj_idx", [P, T, NC], I32)

        ring = work[:, 0:4 * 4096].rearrange("p (q m n) -> p q m n", q=NQ, m=MQ)
        selfterm = work[:, 16384:20480].rearrange("p (t f) -> p t f", t=T)
        degp = work[:, 20480:22528].rearrange("p (q n) -> p q n", q=NQ)
        upd = work[:, 22528:23040].rearrange("p (t f) -> p t f", t=TB)
        upd2 = work[:, 23040:23552].rearrange("p (t f) -> p t f", t=TB)
        inv = work[:, 23552:23556]
        ag = work[:, 30728:31240].rearrange("p (c n) -> p c n", c=QC)
        onehot = work[:, 23560:27656].bitcast(BF16).rearrange("p (b s m) -> p b s m", b=2, s=P)
        coded = work[:, 27656:30728].bitcast(BF16).rearrange("p (b v c m) -> p b v c m", b=2, v=3, c=NC)
        ac = work[:, 0:1536].rearrange("p (b c n) -> p b c n", b=NBUF, c=QC)
        hg1 = work[:, 1536:3084].rearrange("p (b c f) -> p b c f", b=NBUF, c=QC)
        hg2 = work[:, 1536:3072].rearrange("p (b c f) -> p b c f", b=NBUF, c=QC)
        kvg = work[:, 1536:4608].rearrange("p (b c f) -> p b c f", b=NBUF, c=QC)
        neg = work[:, 4608:5120]
        lgT = work[:, 5120:6656].rearrange("p (b c n) -> p b c n", b=NBUF, c=QC)
        e = work[:, 6656:12800].rearrange("p (b h m) -> p b h m", b=NBUF, h=H)
        e1 = e[:, :, 0, :]
        eT = work[:, 12800:14848].rearrange("p (c h n) -> p c h n", c=QC, h=H)
        kT = work[:, 14848:15360]
        outT, hmean, sm = (work[:, 15360 + P * n:15360 + P * n + P] for n in range(3))
        qz = work[:, 16384:17920].rearrange("p (b h n) -> p b h n", b=NBUF, h=H)
        junk = work[:, 24704:24832]
        kvrow = work[:, 24832:25344].rearrange("p (b f) -> p b f", b=2)
        acc = work[:, 25344:29568].rearrange("p (t f) -> p t f", t=T + 1)
        fin = work[:, 6656:10752].rearrange("p (v t f) -> p v t f", v=4, t=FT)
        qT = work[:, 20480:24704]
        xr = h_sb

        ps = ctx.enter_context(nc.psum_tensor("ps", [P, 8, 512], F32))

        ld = sem("ld")
        iotas = sem("iotas")
        flag_ready = sem("flag_ready")
        slot_seen = sem("slot_seen")
        place_done = sem("place_done")
        place_read = sem("place_read")
        coded_ready = sem("coded_ready")
        list_done = sem("list_done")
        list_read = sem("list_read")
        link_i = sem("link_i")
        link_t = sem("link_t")
        link_l = sem("link_l")
        link_q = sem("link_q")
        pads = sem("pads")
        ag_all = sem("ag_all")
        padded = sem("padded")
        bounds_ready = sem("bounds_ready")
        staged = {k: sem(f"staged{k}") for k in range(4)}
        ag_full = [sem("ag_full0"), sem("ag_full1")]
        ag_stored = [sem("ag_stored0"), sem("ag_stored1")]
        qv_ready = sem("qv_ready")
        qv_done = sem("qv_done")
        tables_ready = sem("tables_ready")
        row_stored = {k: [sem(f"row_stored{k}_{b}") for b in range(2)] for k in (1, 2, 3)}
        ac_full = {k: [sem(f"ac_full{k}_{b}") for b in range(NBUF)] for k in (1, 2, 3)}
        hg_full = {k: [sem(f"hg_full{k}_{b}") for b in range(NBUF)] for k in (1, 2, 3)}
        link_a = sem("link_a")
        link_e = {k: sem(f"link_e{k}") for k in (1, 2, 3)}
        state_reset = {k: sem(f"state_reset{k}") for k in (1, 2, 3)}
        mean_done = sem("mean_done")
        lgT_ready = sem("lgT_ready")
        lg_done = sem("lg_done")
        mx_ready = {k: sem(f"mx_ready{k}") for k in (1, 3)}
        e_ready = {k: sem(f"e_ready{k}") for k in (1, 3)}
        al_ready = {k: sem(f"al_ready{k}") for k in (1, 3)}
        eT_done = {k: sem(f"eT_done{k}") for k in (1, 3)}
        eT_out = {k: sem(f"eT_out{k}") for k in (1, 3)}
        eT_outd = sem("eT_outd")
        pv_done = {k: sem(f"pv_done{k}") for k in (1, 2, 3)}
        pv_read = {k: sem(f"pv_read{k}") for k in (1, 2, 3)}
        w_done = sem("w_done")
        w_read = sem("w_read")
        agg_ready = sem("agg_ready")
        summed2 = sem("summed2")
        stat_done2 = sem("stat_done2")
        qz_ready = sem("qz_ready")
        kT_done = sem("kT_done")
        kT_out = sem("kT_out")
        agT_done = sem("agT_done")
        neg_ready = sem("neg_ready")
        s_done = sem("s_done")
        s_read = sem("s_read")
        oT_out = sem("oT_out")
        o_done = sem("o_done")
        z_ready = sem("z_ready")
        ez_ready = sem("ez_ready")
        fin_out = sem("fin_out")
        cst = sem("cst")
        block = ctx.enter_context(nc.Block())

        stat_done = [sem(f"stat_done{k}") for k in range(2)]
        ln_ready = [sem(f"ln_ready{k}") for k in range(4)]
        var_ready = [sem(f"var_ready{k}") for k in range(4)]
        std_ready = [sem(f"std_ready{k}") for k in range(4)]
        ht_ready = [sem(f"ht_ready{k}") for k in range(4)]
        tr_done = {k: sem(f"tr_done{k}") for k in (0, 2, 3)}
        hT_ready = {k: sem(f"hT_ready{k}") for k in (0, 2, 3)}
        proj_done = {k: sem(f"proj_done{k}") for k in (0, 2, 3)}
        post_done = [sem(f"post_done{k}") for k in range(4)]
        slot_full = [sem(f"slot_full{q}") for q in range(NQ)]
        slot_used = [sem(f"slot_used{q}") for q in range(NQ)]
        slot_summed = [sem(f"slot_summed{q}") for q in range(NQ)]
        agg_done = sem("agg_done")
        agg_out = sem("agg_out")
        up_done = sem("up_done")
        up_used = sem("up_used")
        deg_done = sem("deg_done")
        primed = [flag_ready, flag_ready, slot_seen, agg_out, up_used, up_done, deg_done, place_read,
                  list_read, list_read, list_done, list_done, kT_done, kT_out, agT_done, neg_ready, s_done, s_read, w_done, w_read,
                  oT_out, o_done, agg_ready, lgT_ready, lg_done, qz_ready, eT_outd]
        for k in (1, 2, 3):
            primed += [pv_done[k], pv_done[k], pv_read[k], pv_read[k], state_reset[k]]
        for k in (1, 3):
            primed += [mx_ready[k], e_ready[k], e_ready[k], al_ready[k], eT_done[k], eT_out[k]]

        link_ln = [sem(f"link_ln{k}") for k in range(4)]
        link_up = sem("link_up")
        link_m = {k: sem(f"link_m{k}") for k in (1, 3)}
        link_u = sem("link_u")
        ht_copied = sem("ht_copied")
        NLD = 16

        def wait(eng, s, value):
            if isinstance(value, int) and value <= 0:
                return
            eng.wait_ge(s, value)

        def settle(eng):
            eng.nop(nofuse=True)

        def each_tile(eng, body, n=T):
            body(0, 0)
            body(1, 1)
            with eng.Fori(1, n // 2) as i:
                body(2 * i, 0)
                body(2 * i + 1, 1)

        def overlapped(eng, head, tail, n=T):
            head(0, 0)
            head(1, 1)
            tail(0, 0)
            head(2, 0)
            tail(1, 1)
            with eng.Fori(1, n // 2 - 1) as i:
                head(2 * i + 1, 1)
                tail(2 * i, 0)
                head(2 * i + 2, 0)
                tail(2 * i + 1, 1)
            head(n - 1, 1)
            tail(n - 2, 0)
            tail(n - 1, 1)

        class Quad:
            def __init__(self, turn, b):
                self.turn, self.b, self.q = turn + b // NBUF, b % NBUF, NBUF * turn + b

            def ahead(self, n):
                turn = self.turn + (self.b + n) // NBUF if (self.b + n) // NBUF else self.turn
                return Quad(turn, (self.b + n) % NBUF)

        def each_quad(eng, body):
            last = eng.value_load(stepsi[0:1, 0:1], min_val=1, max_val=STEPS)
            with eng.Fori(0, last) as i:
                for b in range(NBUF):
                    body(Quad(i, b))
            return last

        def adj_loaded(eng, k, g):
            eng.wait_ge(ac_full[k][g.b], 16 * (g.turn + 1))

        def nodes_gathered(eng, k, g):
            eng.wait_ge(hg_full[k][g.b], 16 * QC * (g.turn + 1))

        def quad_value(eng, table, q, most):
            return eng.value_load(table[0:1, bass.ds(q, 1)], min_val=0, max_val=most)

        class Link:
            def __init__(self, dve, s, per, turn=0):
                self.dve, self.s, self.per, self.base, self.n = dve, s, per, per * turn, 0

            def __call__(self, ins):
                self.n += 1
                assert self.n <= self.per
                ins.then_inc(self.s, 1)
                self.dve.wait_ge(self.s, self.base + self.n)
                settle(self.dve)

            def end(self):
                assert self.n == self.per, self.n

        @block.sync
        def _(sp):
            sp.dma_start(x_sb[:, :, :], x.rearrange("(t p) f -> p t f", p=P)).then_inc(ld, 16)
            for dst, src in ((k0_sb[:, :], k0), (w2_sb[:, :, :], w2.rearrange("(a f) o -> f a o", a=2)),
                             (hv_bc[:, :], hv.rearrange("f a -> a f").to_broadcast([P, P])),
                             (beta_sb[:, :], beta.rearrange("(t p) -> p t", p=P)),
                             (wq_sb[:, :], wq), (bq_sb[:, :], bq.rearrange("(p a) -> p a", a=1)),
                             (b0_bc[:, :], b0.rearrange("(a f) -> a f", a=1).to_broadcast([P, P])),
                             (b2_bc[:, :], b2.rearrange("(a f) -> a f", a=1).to_broadcast([P, P])),
                             (wb_bc[:, :], wb.rearrange("f a -> a f").to_broadcast([P, 3 * P]))):
                with nc.allow_non_contiguous_dma(reason="small constants"):
                    sp.dma_start(dst, src).then_inc(ld, 16)
            for j, (w, b) in enumerate(zip(wkvs, bkvs)):
                sp.dma_start(wkvs_sb[:, j * P:(j + 1) * P], w).then_inc(ld, 16)
                sp.dma_start(bkvs_bc[:, j * P:(j + 1) * P],
                             b.rearrange("(a f) -> a f", a=1).to_broadcast([P, P])).then_inc(ld, 16)

            def block_rows(nb, q):
                return adj_rows[bass.ds(nb * (P * T * TB), P * T * TB), :].rearrange(
                    "(p m t) n -> p m (t n)", p=P, m=T)[:, q * MQ:(q + 1) * MQ, :]

            for q in range(NQ):
                sp.dma_start(ring[:, q, :, :], block_rows(0, q)).then_inc(slot_full[q], 16)
            with sp.Fori(1, NB) as nb:
                for q in range(NQ):
                    sp.wait_ge(slot_used[q] if q < NQ - 1 else agg_done, nb)
                    sp.wait_ge(slot_summed[q], nb)
                    settle(sp)
                    if q < NQ - 1:
                        sp.wait_ge(slot_seen, SEEN * nb - SEEN + 2 * q + 3)
                    sp.dma_start(ring[:, q, :, :], block_rows(nb, q)).then_inc(slot_full[q], 16)

            sp.wait_ge(cst, 7)
            for table, width in ((h1_table, P + 1), (h2_table, P), (kv_table, 2 * P)):
                for lo in range(0, width, P):
                    hi = min(width, lo + P)
                    sp.dma_start(table[N:N + 1, lo:hi], zeros[0:1, 0:hi - lo]).then_inc(pads, 16)

            def store_rows(k):
                table, row, ready = {1: (h1_table, h_t[:, :, :], post_done[1]),
                                     2: (h2_table, h_t[:, :, 0:P], ht_ready[2]),
                                     3: (kv_table, kvrow, post_done[3])}[k]
                with sp.Fori(0, T // 2) as i:
                    for b in range(2):
                        sp.wait_ge(ready, 2 * i + b + 1)
                        sp.dma_start(table[bass.ds((2 * i + b) * P, P), :], row[:, b, :]).then_inc(row_stored[k][b], 16)

            def adj_read(eng, k, q):
                s, n = {1: (lgT_ready, 1), 2: (pv_done[2], 2), 3: (agT_done, 1)}[k]
                eng.wait_ge(s, q + n)

            def load_adj(k):
                def load(g):
                    q, b = g.q, g.b
                    sp.dma_start(ac[:, b, :, :], adj_table[bass.ds(q * P, P), :]
                                 .rearrange("p (c n) -> p c n", c=QC)).then_inc(ac_full[k][b], 16)

                def step(g):
                    adj_read(sp, k, g.q)
                    load(g.ahead(NBUF - 1))
                for b in range(NBUF - 1):
                    load(Quad(0, b))
                steps = each_quad(sp, step)
                for b in range(NBUF - 1):
                    adj_loaded(sp, k, Quad(steps, b))
                    settle(sp)

            store_rows(1)
            sp.wait_ge(tables_ready, 1)
            sp.wait_ge(ag_all, 1)
            load_adj(1)
            store_rows(2)
            load_adj(2)
            store_rows(3)
            load_adj(3)
            with sp.Fori(0, 4) as i:
                sp.wait_ge(link_e[3], 15 * i + 15)
                sp.dma_start(out[bass.ds(i * (N // 4), N // 4), :].rearrange("(t p) f -> p t f", p=P),
                             x_sb[:, bass.ds(8 * i, 8), :]).then_inc(fin_out, 16)
            sp.wait_ge(fin_out, 64)

        @block.gpsimd
        def _(pool):
            for s in primed:
                pool.sem_inc(s, 1)
            nc.gpsimd.iota(iota_s[:, :, :], [[1, P], [0, T]], 0, 0, True).then_inc(iotas, 1)
            nc.gpsimd.iota(iota_c[:, :, :], [[1, NC], [0, T]], 0, 0, True).then_inc(iotas, 1)
            nc.gpsimd.iota(iota_m[:, :], [[1, T]], 0, 0, True).then_inc(iotas, 1)
            nc.gpsimd.iota(iota_p[:, :], [[1, 1]], 0, 1, True).then_inc(iotas, 1)
            nc.gpsimd.iota(iota_j[:, :, :], [[0, TB], [QW, NP]], 0, 0, True).then_inc(iotas, 1)
            nc.gpsimd.iota(row0[:, :], [[P * T * TB, NB], [1, TB]], -ZERO_ROW, 0, True).then_inc(iotas, 1)
            nc.gpsimd.iota(qnum[:, :], [[P, 3]], 0, 1, True).then_inc(iotas, 1)
            nc.gpsimd.iota(step_at[:, :], [[NBUF, STEPS]], 0, 0, True).then_inc(iotas, 1)
            nc.gpsimd.memset(ones_b[:, :], 1.0).then_inc(iotas, 1)
            nc.gpsimd.memset(tri[:, :], 1.0).then_inc(iotas, 1)
            nc.gpsimd.memset(gate[:, :, :], 1.0).then_inc(iotas, 1)
            pool.wait_ge(iotas, 11)
            nc.gpsimd.memset(gate[:, :, 0:1], 0.0).then_inc(iotas, 1)
            nc.gpsimd.affine_select(out=tri[:, :], in_=tri[:, :], compare_op=ALU.is_gt, fill=0.0,
                                    base=0, pattern=[[1, P]], channel_multiplier=-1).then_inc(iotas, 1)
            nc.gpsimd.memset(ident[:, :], 0.0).then_inc(cst, 1)
            nc.gpsimd.memset(ones[:, :], 1.0).then_inc(cst, 1)
            nc.gpsimd.memset(zeros[:, :], 0.0).then_inc(cst, 1)
            nc.gpsimd.memset(hmask[:, :], 1.0).then_inc(cst, 1)
            pool.wait_ge(cst, 4)
            nc.gpsimd.affine_select(out=ident[:, :], in_=ident[:, :], compare_op=ALU.not_equal, fill=1.0,
                                    base=0, pattern=[[-1, P]], channel_multiplier=1).then_inc(cst, 1)
            nc.gpsimd.affine_select(out=hmask[:, :], in_=hmask[:, :], compare_op=ALU.is_ge, fill=0.0,
                                    base=0, pattern=[[-C, H]], channel_multiplier=1).then_inc(cst, 1)
            pool.wait_ge(cst, 6)
            nc.gpsimd.affine_select(out=hmask[:, :], in_=hmask[:, :], compare_op=ALU.is_ge, fill=0.0,
                                    base=C - 1, pattern=[[C, H]], channel_multiplier=-1).then_inc(cst, 1)

            nc.gpsimd.memset(node_idx[:, T, :], N).then_inc(padded, 1)
            nc.gpsimd.memset(ag[:, :, :], 0.0).then_inc(padded, 1)
            pool.wait_ge(padded, 2)

            def store_half(q, half, rows):
                pool.dma_start(adj_table[bass.ds(q * P, P), half * HALF * P:(half + 1) * HALF * P]
                               .rearrange("p (c n) -> p c n", c=HALF), rows).then_inc(ag_stored[half], 16)

            for half in range(2):
                store_half(QUADS + BEHIND, half, ag[:, half * HALF:(half + 1) * HALF, :])

            def gather_adj(t, first):
                end = pool.value_load(bounds[0:1, bass.ds(t + 1, 1)], min_val=1, max_val=QUADS)
                with pool.Fori(first, end) as q:
                    j = nc.s_assert_within(q - first, 0, NP - 1,
                                           skip_runtime_bounds_check_because="a tile has at most N neighbours")
                    nc.gpsimd.tensor_copy(stage[:, 0, :], adj_idx[:, bass.ds(t, 1), bass.ds(QC * j, QC)]
                                          .rearrange("p a c -> p (a c)")).then_inc(staged[0], 1)
                    pool.wait_ge(staged[0], q + 1)
                    for half in range(2):
                        pool.wait_ge(ag_stored[half], 16 * q + 16)
                        settle(pool)
                        for c in range(half * HALF, (half + 1) * HALF):
                            nc.gpsimd.indirect_dma_start(
                                out=ag[:, c, :], out_offset=None, in_=adj_rows,
                                in_offset=bass.IndirectOffsetOnAxis(ap=stage[:, 0, c:c + 1], axis=0)).then_inc(ag_full[half], 16)
                    for half in range(2):
                        pool.wait_ge(ag_full[half], 32 * q + 32)
                        settle(pool)
                        store_half(q, half, ag[:, half * HALF:(half + 1) * HALF, :])
                return end

            with pool.Fori(0, NB) as nb:
                pool.wait_ge(list_read, nb * TB + TB + 2)
                settle(pool)
                end = pool.value_load(bounds[0:1, bass.ds(nb * TB, 1)], min_val=0, max_val=QUADS)
                for j in range(TB):
                    end = gather_adj(nb * TB + j, end)
            last = pool.value_load(bounds[0:1, T:T + 1], min_val=1, max_val=QUADS)
            for n in range(BEHIND):
                for half in range(2):
                    store_half(last + n, half, zeros[:, :].rearrange("p (a n) -> p a n", a=1).to_broadcast([P, HALF, P]))
            for half in range(2):
                pool.wait_ge(ag_stored[half], 16 * last + 16 * (BEHIND + 1))
                settle(pool)
            pool.sem_inc(ag_all, 1)

            def gather_nodes(k):
                rows, table = {1: (hg1, h1_table), 2: (hg2, h2_table), 3: (kvg, kv_table)}[k]

                def gather(g):
                    q, b = g.q, g.b
                    column = quad_value(pool, quad_col, q, T * NC)
                    nc.gpsimd.tensor_copy(stage[:, b, :], node_idx[:, :, :].rearrange("p t c -> p (t c)")[:, bass.ds(column, QC)]
                                          ).then_inc(staged[k], 1)
                    pool.wait_ge(staged[k], q + 1)
                    settle(pool)
                    for c in range(QC):
                        nc.gpsimd.indirect_dma_start(
                            out=rows[:, b, c, :], out_offset=None, in_=table,
                            in_offset=bass.IndirectOffsetOnAxis(ap=stage[:, b, c:c + 1], axis=0)).then_inc(hg_full[k][b], 16)

                def step(g):
                    pool.wait_ge(pv_done[k], g.q + 2)
                    settle(pool)
                    gather(g.ahead(NBUF - 1))
                pool.wait_ge(tables_ready, 1)
                for b in range(2):
                    pool.wait_ge(row_stored[k][b], 16 * (T // 2))
                for b in range(NBUF - 1):
                    gather(Quad(0, b))
                steps = each_quad(pool, step)
                for b in range(NBUF - 1):
                    nodes_gathered(pool, k, Quad(steps, b))
                    settle(pool)

            pool.wait_ge(pads, 16 * 5)
            for k in (1, 2, 3):
                gather_nodes(k)

        @block.scalar
        def _(act):
            def normalise(k):
                act.wait_ge(var_ready[k], 1)
                nc.scalar.activation(lnw[:, 3, :], lnw[:, 2, :], ACT.Sqrt).then_inc(std_ready[k], 1)
                act.wait_ge(ln_ready[k], 1)

                def relu(t, b):
                    if k in (0, 2, 3):
                        wait(act, tr_done[k], t - 1)
                    if k == 0:
                        wait(act, ht_copied, t - 1)
                    if k == 1:
                        wait(act, mean_done, t - 1)
                    if k in (1, 2) and not isinstance(t, int):
                        act.wait_ge(row_stored[k][b], 8 * (t - b))
                    nc.scalar.activation(h_t[:, b, 0:P], x_sb[:, t, :], ACT.Relu, bias=nmean[:, bass.ds(t, 1)],
                                         scale=rstd[:, bass.ds(t, 1)]).then_inc(ht_ready[k], 1)
                each_tile(act, relu)

            def use_exp():
                nc.scalar.activation(tiny[:, 0:1], ones[:, 0:1], ACT.Exp)

            normalise(0)
            def see(nb, b):
                act.wait_ge(flag_ready, nb + 1)
                for q in range(NQ - 1):
                    act.wait_ge(slot_full[q], 16 * nb + 16)
                    for half in range(2):
                        act.wait_ge(slot_seen, SEEN * nb + 2 * q + half + 1)
                        settle(act)
                        for m in range(MQ // 2 * half, MQ // 2 * (half + 1)):
                            for t in range(TB):
                                ins = nc.scalar.activation(unread[:, m % (MQ // 2) * TB + t, :],
                                                           ring[:, q, m, t * P:(t + 1) * P], ACT.Abs,
                                                           accum_out=seen[:, b, t, q * MQ + m:q * MQ + m + 1])
                        ins.then_inc(slot_seen, 1)

            with act.Fori(0, NB // 2) as i:
                see(2 * i, 0)
                see(2 * i + 1, 1)
            normalise(1)

            grown, nbest, alpha, part = (sm[:, 3 + NBUF * n:3 + NBUF * n + NBUF] for n in range(1, 5))

            def exps1(g):
                q, b = g.q, g.b
                act.wait_ge(mx_ready[1], q + 2)
                act.wait_ge(eT_done[1], q + 1)
                act.wait_ge(pv_read[1], q + 1)
                nc.scalar.activation(alpha[:, b:b + 1], grown[:, b:b + 1], ACT.Exp).then_inc(al_ready[1], 1)
                nc.scalar.activation(e1[:, b, :], ps[:, b, :], ACT.Exp, bias=nbest[:, b:b + 1],
                                     accum_out=part[:, b:b + 1]).then_inc(e_ready[1], 1)

            def turned1(g):
                act.wait_ge(eT_done[1], g.q + 2)
                act.wait_ge(pv_done[1], g.q + 2)
                nc.scalar.activation(eT[:, :, 0, :], ps[:, 3, :].rearrange("p (c n) -> p c n", c=QC),
                                     ACT.Copy).then_inc(eT_out[1], 1)

            def step1(g):
                turned1(g)
                exps1(g.ahead(1))

            use_exp()
            act.wait_ge(tables_ready, 1)
            exps1(Quad(0, 0))
            each_quad(act, step1)

            normalise(2)

            act.wait_ge(summed2, 1)
            with act.Fori(0, NB) as nb:
                act.wait_ge(w_done, nb + 1)
                settle(act)
                nc.scalar.activation(aggT[:, :], acc[:, bass.ds(nb * TB, TB), :].rearrange("p t f -> p (t f)"),
                                     ACT.Copy).then_inc(agg_ready, 1)

            normalise(3)

            def keys(g):
                q, b = g.q, g.b
                act.wait_ge(kT_done, q + 2)
                act.wait_ge(s_done, H * q + 1)
                nc.scalar.activation(kT[:, :], ps[:, 0, :], ACT.Copy).then_inc(kT_out, 1)

            grown3, nbest3, alpha3, part3 = (sm[:, 12 * n + 12:12 * n + 24].rearrange("p (b h) -> p b h", b=NBUF)
                                             for n in range(1, 5))

            def exps3(g, heads):
                q, b = g.q, g.b
                if 0 in heads:
                    act.wait_ge(mx_ready[3], q + 2)
                    act.wait_ge(pv_read[3], q + 1)
                    nc.scalar.activation(alpha3[:, b, :], grown3[:, b, :], ACT.Exp, scale=SCALE).then_inc(al_ready[3], 1)
                for h in heads:
                    nc.scalar.activation(e[:, b, h, :], e[:, b, h, :], ACT.Exp, bias=nbest3[:, b, h:h + 1],
                                         scale=SCALE, accum_out=part3[:, b, h:h + 1]).then_inc(e_ready[3], 1)

            def step3(g):
                q = g.q
                for c in (0, 2):
                    act.wait_ge(eT_done[3], QC * q + c + 2)
                    act.wait_ge(pv_done[3], q + 2)
                    nc.scalar.activation(eT[:, c, :, :], ps[:, 5, :].rearrange("p (h n) -> p h n", h=H),
                                         ACT.Copy).then_inc(eT_out[3], 1)
                exps3(g.ahead(1), (0, 1))
                act.wait_ge(pv_done[3], q + 3)
                act.wait_ge(o_done, q + 1)
                nc.scalar.activation(outT[:, :], ps[:, 7, 0:P], ACT.Copy).then_inc(oT_out, 1)
                keys(g.ahead(2))
                exps3(g.ahead(1), (2, 3))

            use_exp()
            keys(Quad(0, 0))
            exps3(Quad(0, 0), range(H))
            keys(Quad(0, 1))
            each_quad(act, step3)
            with act.Fori(0, T // FT) as i:
                act.wait_ge(z_ready, i + 1)
                nc.scalar.activation(zed[:, :, :], zed[:, :, :], ACT.Exp, scale=-1.0).then_inc(ez_ready, 1)

        @block.vector
        def _(dve):
            dve.wait_ge(ld, 16 * NLD)
            dve.wait_ge(cst, 7)
            dve.wait_ge(iotas, 13)

            def row_stats(k, nb):
                for j in range(TB):
                    ins = nc.vector.bn_stats(stats[:, TB * nb + j, :], x_sb[:, TB * nb + j, :])
                ins.then_inc(stat_done[k], 1)

            def moments(k, count):
                if count is not None:
                    dve.wait_ge(stat_done[k], count)
                link = Link(dve, link_ln[k], 8)
                a, d, v, sd = (lnw[:, n, :] for n in range(4))
                me, mo, ve, vo = (stats[:, :, n] for n in (1, 4, 2, 5))
                link(nc.vector.tensor_tensor(d, me, mo, ALU.subtract))
                link(nc.vector.tensor_tensor(a, ve, vo, ALU.add))
                link(nc.vector.tensor_tensor(d, d, d, ALU.mult))
                link(nc.vector.tensor_scalar(a, a, 1.0 / P, EPS, ALU.mult, ALU.add))
                link(nc.vector.scalar_tensor_tensor(v, d, 0.25, a, ALU.mult, ALU.add))
                nc.vector.tensor_tensor(a, me, mo, ALU.add).then_inc(var_ready[k], 1)
                dve.wait_ge(var_ready[k], 1)
                dve.wait_ge(std_ready[k], 1)
                link(nc.vector.reciprocal(rstd[:, :], sd))
                link(nc.vector.scalar_tensor_tensor(nmean[:, :], a, -0.5, rstd[:, :], ALU.mult, ALU.mult))
                link(nc.vector.tensor_copy(lnw[:, 1, :], rstd[:, :]))
                link.end()
                nc.vector.tensor_copy(lnw[:, 0, :], nmean[:, :]).then_inc(ln_ready[k], 1)

            def node_terms(k):
                def score(t, b):
                    dve.wait_ge(ht_ready[1], t + 1)
                    wait(dve, post_done[1], t)
                    nc.vector.tensor_tensor_reduce(out=junk, in0=h_t[:, b, 0:P], in1=hv_bc[:, :], scale=1.0,
                                                   scalar=0.0, op0=ALU.mult, op1=ALU.add,
                                                   accum_out=h_t[:, b, P:P + 1]).then_inc(post_done[1], 1)

                def features(t, b):
                    dve.wait_ge(ht_ready[k], t + 1)
                    if k == 0:
                        nc.vector.tensor_copy(h_sb[:, t, :], h_t[:, b, 0:P]).then_inc(ht_copied, 1)
                    dve.wait_ge(tr_done[k], t + 1)
                    wait(dve, proj_done[k], t - 1)
                    nc.vector.tensor_copy(hT[:, b, :], ps[:, b, 0:P]).then_inc(hT_ready[k], 1)

                def products(t, b):
                    dve.wait_ge(proj_done[k], t + 1)
                    got = ps[:, 2 + b, 0:P]
                    if k == 0:
                        ins = nc.vector.tensor_scalar(selfterm[:, t, :], got, beta_sb[:, bass.ds(t, 1)], None, ALU.mult)
                    elif k == 2:
                        ins = nc.vector.tensor_tensor(selfterm[:, t, :], got, b2_bc[:, :], ALU.add)
                    else:
                        if not isinstance(t, int) or t > 1:
                            dve.wait_ge(row_stored[3][b], 8 * (t - b))
                        nc.vector.tensor_tensor(kvrow[:, b, :], ps[:, 2 + b, 0:2 * P], bkvs_bc[:, 0:2 * P], ALU.add)
                        nc.vector.tensor_tensor(xr[:, t, :], ps[:, 2 + b, 2 * P:3 * P], bkvs_bc[:, 2 * P:3 * P], ALU.add)
                        ins = nc.vector.tensor_scalar(qT[:, bass.ds(t * P, P)], ps[:, 4 + b, 0:P], bq_sb[:, 0:1],
                                                      None, ALU.add)
                    ins.then_inc(post_done[k], 1)

                if k == 1:
                    each_tile(dve, score)
                else:
                    overlapped(dve, features, products)

            def seen_of(nb):
                return seen[:, bass.ds(nb % 2, 1), :, :].rearrange("p a t m -> p (a t) m")

            def mark(nb):
                dve.wait_ge(slot_seen, SEEN * nb + SEEN + 1)
                dve.wait_ge(slot_summed[NQ - 1], nb + 1)
                nc.vector.tensor_scalar(flag[:, :, :], seen_of(nb)[:, :, :], 0.0, None, ALU.not_equal).then_inc(flag_ready, 1)

            def place(nb):
                link = Link(dve, link_i, 14, nb)
                dve.wait_ge(place_done, nb + 1)
                before, of_tile = (ps[:, 5, 128 * n + 128:128 * n + 256] for n in range(2))
                flat = (lambda a: a[:, :, :].rearrange("p t m -> p (t m)"))
                link(nc.vector.tensor_tensor_scan(flat(run), flat(gate), of_tile, 0.0, ALU.mult, ALU.add))
                link(nc.vector.tensor_tensor(flat(pos), flat(run), of_tile, ALU.subtract))
                nc.vector.tensor_tensor(flat(pos), flat(pos), before, ALU.add).then_inc(place_read, 1)
                dve.wait_ge(place_read, nb + 2)
                link(nc.vector.scalar_tensor_tensor(flat(pos), flat(flag), -2.0 * N, flat(pos), ALU.mult, ALU.add))
                link(nc.vector.tensor_scalar(flat(posi), flat(pos), 2.0 * N, None, ALU.add))
                link(nc.vector.tensor_scalar(flat(sloti), flat(posi), P - 1, None, ALU.bitwise_and))
                link(nc.vector.tensor_copy(flat(slot), flat(sloti)))
                link(nc.vector.tensor_scalar(flat(sloti), flat(posi), 7, None, ALU.logical_shift_right))
                link(nc.vector.tensor_copy(flat(chunk), flat(sloti)))
                link(nc.vector.tensor_tensor(more[:, :, :], run[:, :, T - 1:T].to_broadcast([P, TB, NP]),
                                             iota_j[:, :, :], ALU.is_gt))
                link(nc.vector.tensor_reduce(quads[:, :], more[:, :, :], AX.X, ALU.add))
                link(nc.vector.tensor_scalar(quads[:, :], quads[:, :], 1.0, None, ALU.max))
                link(nc.vector.tensor_copy(last_end[:, :], ends[:, bass.ds(nb * TB, 1)]))
                link(nc.vector.tensor_tensor_scan(ends4[:, :], ones[:, 0:TB], quads[:, :], last_end[:, 0:1],
                                                  ALU.mult, ALU.add))
                nc.vector.tensor_copy(ends[:, bass.ds(nb * TB + 1, TB)], ends4[:, :])
                link(nc.vector.tensor_copy(bounds[:, bass.ds(nb * TB + 1, TB)], ends4[:, :]))
                link.end()

            def code(nb, j):
                b = j % 2
                n = nb * TB + j
                dve.wait_ge(list_done, n + 1)
                nc.vector.tensor_tensor(onehot[:, b, :, :], iota_s[:, :, :], slot[:, j:j + 1, :]
                                        .to_broadcast([P, P, T]), ALU.is_equal)
                nc.vector.tensor_tensor(coded[:, b, 2, :, :], iota_c[:, :, :], chunk[:, j:j + 1, :]
                                        .to_broadcast([P, NC, T]), ALU.is_equal).then_inc(link_t, 1)
                dve.wait_ge(link_t, n + 1)
                nc.vector.tensor_tensor(coded[:, b, 0, :, :], coded[:, b, 2, :, :], iota_m[:, :]
                                        .rearrange("p (a m) -> p a m", a=1).to_broadcast([P, NC, T]), ALU.mult)
                nc.vector.tensor_scalar(coded[:, b, 1, :, :], coded[:, b, 2, :, :], iota_p[:, 0:1], None,
                                        ALU.mult).then_inc(coded_ready, 1)

            def lists(nb, j):
                n = nb * TB + j
                link = Link(dve, link_l, 4, n)
                dve.wait_ge(list_read, n + 2)
                dve.wait_ge(list_done, n + 3)
                got = ps[:, 7 if j % 2 else 3, 0:3 * NC].rearrange("p (v c) -> p v c", v=3)
                link(nc.vector.tensor_scalar(idxf[:, 0, :], got[:, 2, :], -float(N), float(N), ALU.mult, ALU.add))
                link(nc.vector.scalar_tensor_tensor(idxf[:, 0, :], got[:, 0, :], float(P), idxf[:, 0, :], ALU.mult, ALU.add))
                link(nc.vector.tensor_scalar(idxf[:, 1, :], got[:, 2, :], row0[:, bass.ds(n, 1)], float(ZERO_ROW),
                                             ALU.mult, ALU.add))
                link(nc.vector.scalar_tensor_tensor(idxf[:, 1, :], got[:, 0, :], float(TB), idxf[:, 1, :], ALU.mult, ALU.add))
                nc.vector.tensor_tensor(node_idx[:, n, :], idxf[:, 0, :], got[:, 1, :], ALU.add)
                nc.vector.scalar_tensor_tensor(adj_idx[:, n, :], got[:, 1, :], float(T * TB), idxf[:, 1, :], ALU.mult,
                                               ALU.add).then_inc(list_read, 1)
                link.end()

            def number_quads():
                link = Link(dve, link_q, 16)
                ends_in = ends[:, 1:T + 1].rearrange("p (a t) -> p a t", a=1).to_broadcast([P, 3, T])
                nums = qnum[:, :].rearrange("p (c a) -> p c a", a=1).to_broadcast([P, 3, T])
                tile, begin, col = (qval[:, n, :] for n in range(3))
                link(nc.vector.tensor_tensor(qcmp[:, :, :], ends_in, nums, ALU.is_le))
                link(nc.vector.tensor_reduce(tile, qcmp[:, :, :], AX.X, ALU.add))
                link(nc.vector.tensor_tensor(qcmp[:, :, :], ends_in, qcmp[:, :, :], ALU.mult))
                link(nc.vector.tensor_reduce(begin, qcmp[:, :, :], AX.X, ALU.max))
                link(nc.vector.tensor_tensor(col, qnum[:, :], begin, ALU.subtract))
                link(nc.vector.tensor_scalar(col, col, float(QC), None, ALU.mult))
                link(nc.vector.scalar_tensor_tensor(col, tile, float(NC), col, ALU.mult, ALU.add))
                link(nc.vector.tensor_scalar(col, col, float(T * NC), None, ALU.min))
                link(nc.vector.tensor_scalar(tile, tile, float(T), None, ALU.min))
                first = begin
                link(nc.vector.tensor_tensor(first, qnum[:, :], begin, ALU.is_equal))
                for n, (v, table) in enumerate(((col, quad_col), (tile, quad_tile), (first, quad_first))):
                    if n:
                        dve.wait_ge(qv_done, n)
                    for c in range(3):
                        ins = nc.vector.tensor_scalar(qdiag[:, c, :], ident[:, :], v[:, c:c + 1], None, ALU.mult)
                    ins.then_inc(qv_ready, 1)
                    dve.wait_ge(qv_done, n + 1)
                    link(nc.vector.tensor_copy(table[:, :], ps[:, 1, 0:3 * P]))
                link(nc.vector.tensor_scalar(cap[:, :], quad_first[:, :], LOW - HIGH, HIGH, ALU.mult, ALU.add))
                link(nc.vector.tensor_scalar(step_at[:, :], step_at[:, :], ends[:, T:T + 1], None, ALU.is_lt))
                link(nc.vector.tensor_reduce(steps[:, :], step_at[:, :], AX.X, ALU.add))
                link.end()
                nc.vector.tensor_copy(stepsi[:, :], steps[:, :]).then_inc(tables_ready, 1)
                dve.wait_ge(tables_ready, 1)

            def reduce_slot(nb, q):
                dve.wait_ge(slot_full[q], 16 * nb + 16 if not isinstance(nb, int) else 16 * (nb + 1))
                if q == 0:
                    dve.wait_ge(deg_done, nb + 1)
                ins = nc.vector.tensor_reduce(degp[:, q, :], ring[:, q, :, :].rearrange("p m n -> p n m"), AX.X, ALU.add)
                if q == NQ - 1:
                    ins = nc.vector.tensor_reduce(seen_of(nb)[:, :, q * MQ:(q + 1) * MQ].rearrange("p t m -> p m t"),
                                        ring[:, q, :, :].rearrange("p m (t n) -> p m t n", t=TB), AX.X, ALU.max,
                                        apply_absolute_value=True)
                ins.then_inc(slot_summed[q], 1)

            def update(nb):
                link = Link(dve, link_up, 5, nb)
                xs = x_sb[:, bass.ds(nb * TB, TB), :]
                own = selfterm[:, bass.ds(nb * TB, TB), :]
                got = ps[:, 1, :].rearrange("p (t f) -> p t f", t=TB)
                dve.wait_ge(deg_done, nb + 2)
                link(nc.vector.tensor_tensor(inv, ps[:, 6, 0:TB], beta_sb[:, bass.ds(nb * TB, TB)], ALU.add))
                link(nc.vector.reciprocal(inv, inv))
                dve.wait_ge(up_done, nb + 2)
                nc.vector.tensor_tensor(upd, got, own, ALU.add).then_inc(up_used, 1)
                dve.wait_ge(up_used, nb + 2)
                link(nc.vector.tensor_tensor(upd2, upd, inv.rearrange("p (t a) -> p t a", a=1)
                                             .to_broadcast([P, TB, P]), ALU.mult))
                link(nc.vector.tensor_tensor(upd, upd2, b0_bc[:, :].rearrange("p (a f) -> p a f", a=1)
                                             .to_broadcast([P, TB, P]), ALU.add))
                link(nc.vector.tensor_tensor(xs, upd, xs, ALU.add))
                link.end()
                row_stats(1, nb)

            def block0(nb, last):
                for q in range(NQ):
                    reduce_slot(nb, q)
                    if last is not None and q == 0:
                        place(last)
                    if last is not None:
                        code(last, q)
                        if q:
                            lists(last, q - 1)
                dve.wait_ge(agg_done, nb + 1)
                nc.vector.tensor_copy(aggT[:, :], ps[:, 0, :]).then_inc(agg_out, 1)
                mark(nb)
                update(nb)
                if last is not None:
                    lists(last, TB - 1)

            with dve.Fori(0, NB) as nb:
                row_stats(0, nb)
            moments(0, NB)
            node_terms(0)
            nc.vector.memset(ends[:, 0:1], 0.0)
            nc.vector.memset(bounds[:, 0:1], 0.0).then_inc(bounds_ready, 1)
            dve.wait_ge(bounds_ready, 1)
            block0(0, None)
            with dve.Fori(1, NB) as nb:
                block0(nb, nb - 1)
            place(NB - 1)
            code(NB - 1, 0)
            code(NB - 1, 1)
            lists(NB - 1, 0)
            code(NB - 1, 2)
            lists(NB - 1, 1)
            code(NB - 1, 3)
            lists(NB - 1, 2)
            lists(NB - 1, 3)
            moments(1, NB)
            node_terms(1)
            number_quads()

            want = sm[:, 0:1]
            best, grown, nbest, alpha, part = (sm[:, 3 + NBUF * n:3 + NBUF * n + NBUF] for n in range(5))

            def clear(k):
                if k != 2:
                    nc.vector.memset(sm[:, 3:6] if k == 1 else sm[:, 12:24], 0.0)
                    nc.vector.memset(totals[k][:, :, :], 0.0)
                nc.vector.memset(acc, 0.0).then_inc(state_reset[k], 1)
                dve.wait_ge(state_reset[k], 2)

            def logits(g):
                q, b = g.q, g.b
                adj_loaded(dve, 1, g)
                nodes_gathered(dve, 1, g)
                dve.wait_ge(lgT_ready, q + 1)
                wait(dve, lg_done, q)
                link = Link(dve, link_a, 1, q)
                link(nc.vector.tensor_scalar(neg, ac[:, b, :, :].rearrange("p c n -> p (c n)"), 0.0, NEG,
                                             ALU.is_equal, ALU.mult))
                link.end()
                for c in range(QC):
                    ins = nc.vector.scalar_tensor_tensor(lgT[:, b, c, :], ac[:, b, c, :], hg1[:, b, c, P:P + 1],
                                                         neg[:, c * P:(c + 1) * P], ALU.mult, ALU.add)
                ins.then_inc(lgT_ready, 1)

            def maxima(g):
                q, b = g.q, g.b
                old = best[:, (b - 1) % NBUF:(b - 1) % NBUF + 1]
                capped = cap[:, bass.ds(q, 1)]
                dve.wait_ge(lg_done, q + 2)
                link = Link(dve, link_m[1], 2, q)
                link(nc.vector.tensor_reduce(want, ps[:, b, :], AX.X, ALU.max))
                link(nc.vector.scalar_tensor_tensor(best[:, b:b + 1], old, capped, want, ALU.min, ALU.max))
                link.end()
                nc.vector.scalar_tensor_tensor(grown[:, b:b + 1], old, capped, best[:, b:b + 1], ALU.min, ALU.subtract)
                nc.vector.tensor_scalar(nbest[:, b:b + 1], best[:, b:b + 1], -1.0, None, ALU.mult).then_inc(mx_ready[1], 1)

            def add_up(g):
                q, b = g.q, g.b
                t = quad_value(dve, quad_tile, q, T)
                total = totals[1][:, bass.ds(t, 1), :].rearrange("p t a -> p (t a)")
                dve.wait_ge(al_ready[1], q + 2)
                dve.wait_ge(e_ready[1], q + 3)
                settle(dve)
                nc.vector.scalar_tensor_tensor(total, total, alpha[:, b:b + 1], part[:, b:b + 1], ALU.mult, ALU.add)
                nc.vector.tensor_copy(tops[1][:, bass.ds(t, 1), :].rearrange("p t a -> p (t a)"), best[:, b:b + 1])
                dve.wait_ge(pv_done[1], q + 3)
                settle(dve)
                nc.vector.scalar_tensor_tensor(acc[:, t, :], acc[:, t, :], alpha[:, b:b + 1], ps[:, 4 + b, 0:P], ALU.mult,
                                               ALU.add).then_inc(pv_read[1], 1)
                dve.wait_ge(pv_read[1], q + 3)
                settle(dve)

            def wide(v, f=P):
                return v.to_broadcast([P, FT, f])

            def finish1(i):
                link = Link(dve, link_e[1], 9, i)
                tiles = bass.ds(FT * i, FT)
                r, one = rden[:, :, 0:1], some[:, :, 0:1]
                xs = x_sb[:, tiles, :]
                link(nc.vector.tensor_scalar(r, totals[1][:, tiles, :], TINY, None, ALU.max))
                link(nc.vector.reciprocal(r, r))
                link(nc.vector.tensor_scalar(one, tops[1][:, tiles, :], 0.5 * LOW, None, ALU.is_gt))
                link(nc.vector.tensor_tensor(r, r, one, ALU.mult))
                link(nc.vector.tensor_scalar(one, one, -1.0, 1.0, ALU.mult, ALU.add))
                nc.vector.tensor_tensor(fin[:, 0, :, :], acc[:, tiles, :], wide(r), ALU.mult)
                link(nc.vector.tensor_tensor(fin[:, 1, :, :], hmean.rearrange("p (a f) -> p a f", a=1)
                                             .to_broadcast([P, FT, P]), wide(one), ALU.mult))
                link(nc.vector.tensor_tensor(fin[:, 0, :, :], fin[:, 0, :, :], fin[:, 1, :, :], ALU.add))
                link(nc.vector.tensor_tensor(xs, fin[:, 0, :, :], xs, ALU.add))
                for j in range(FT):
                    ins = nc.vector.bn_stats(stats[:, FT * i + j, :], x_sb[:, FT * i + j, :])
                link(ins)
                link.end()

            def step1(g):
                logits(g.ahead(1))
                maxima(g.ahead(1))
                add_up(g)

            dve.wait_ge(mean_done, T + 1)
            nc.vector.tensor_scalar(hmean, ps[:, 6, 0:P], 1.0 / N, None, ALU.mult).then_inc(post_done[1], 1)
            dve.wait_ge(post_done[1], T + 1)
            clear(1)
            logits(Quad(0, 0))
            maxima(Quad(0, 0))
            end = Quad(each_quad(dve, step1), 0)
            dve.wait_ge(e_ready[1], end.q + 3)
            settle(dve)
            with dve.Fori(0, T // FT) as i:
                finish1(i)
            moments(2, None)
            node_terms(2)

            def step2(g):
                q, b = g.q, g.b
                t = quad_value(dve, quad_tile, q, T)
                dve.wait_ge(pv_done[2], q + 3)
                settle(dve)
                nc.vector.tensor_tensor(acc[:, t, :], acc[:, t, :], ps[:, b, 0:P], ALU.add).then_inc(pv_read[2], 1)
                dve.wait_ge(pv_read[2], q + 3)
                settle(dve)

            clear(2)
            each_quad(dve, step2)
            dve.sem_inc(summed2, 1)
            with dve.Fori(0, NB) as nb:
                link = Link(dve, link_e[2], 1, nb)
                xs = x_sb[:, bass.ds(nb * TB, TB), :]
                dve.wait_ge(w_done, nb + 2)
                nc.vector.tensor_tensor(upd, ps[:, 3, :].rearrange("p (t f) -> p t f", t=TB),
                                        selfterm[:, bass.ds(nb * TB, TB), :], ALU.add).then_inc(w_read, 1)
                dve.wait_ge(w_read, nb + 2)
                settle(dve)
                link(nc.vector.scalar_tensor_tensor(xs, upd, 0.0, xs, ALU.max, ALU.add))
                link.end()
                for j in range(TB):
                    ins = nc.vector.bn_stats(stats[:, nb * TB + j, :], x_sb[:, nb * TB + j, :])
                ins.then_inc(stat_done2, 1)
            dve.wait_ge(stat_done2, NB)
            moments(3, None)
            node_terms(3)

            best3, grown3, nbest3, alpha3, part3, want3 = (
                sm[:, 12 * n + 12:12 * n + 24].rearrange("p (b h) -> p b h", b=NBUF) for n in range(6))
            per_head = (lambda v: v.rearrange("p (h a) -> p h a", a=1).to_broadcast([P, H, C]))

            def queries(g):
                q, b = g.q, g.b
                t = 0 if isinstance(q, int) and q == 0 else quad_value(dve, quad_tile, q, T)
                if not isinstance(q, int):
                    dve.wait_ge(s_done, H * q - 2 * H + 1)
                nc.vector.tensor_tensor(qz[:, b, :, :], qT[:, bass.ds(t * P, P)].rearrange("p (a n) -> p a n", a=1)
                                        .to_broadcast([P, H, P]), hmask[:, :].rearrange("p (h a) -> p h a", a=1)
                                        .to_broadcast([P, H, P]), ALU.mult).then_inc(qz_ready, 1)

            def mask3(g):
                dve.wait_ge(agT_done, g.q + 2)
                dve.wait_ge(s_read, H * g.q + 1)
                nc.vector.tensor_scalar(neg, ps[:, 1, :], 0.0, NEG, ALU.is_equal, ALU.mult).then_inc(neg_ready, 1)
                dve.wait_ge(neg_ready, g.q + 2)

            def scores(g, heads):
                q, b = g.q, g.b
                if not isinstance(q, int):
                    dve.wait_ge(eT_done[3], QC * q - QC + 1)
                for h in heads:
                    dve.wait_ge(s_done, H * q + h + 2)
                    settle(dve)
                    nc.vector.tensor_tensor_reduce(out=e[:, b, h, :], in0=ps[:, 2 + h % 3, :], in1=neg, scale=1.0,
                                                   scalar=-3.0e38, op0=ALU.add, op1=ALU.max,
                                                   accum_out=want3[:, b, h:h + 1]).then_inc(s_read, 1)

            def maxima3(g):
                q, b = g.q, g.b
                old, capped = best3[:, (b - 1) % NBUF, :], cap[:, bass.ds(q, 1)]
                dve.wait_ge(s_read, H * q + H + 1)
                settle(dve)
                link = Link(dve, link_m[3], 1, q)
                link(nc.vector.scalar_tensor_tensor(best3[:, b, :], old, capped, want3[:, b, :], ALU.min, ALU.max))
                link.end()
                nc.vector.scalar_tensor_tensor(grown3[:, b, :], old, capped, best3[:, b, :], ALU.min, ALU.subtract)
                nc.vector.tensor_scalar(nbest3[:, b, :], best3[:, b, :], -SCALE, None, ALU.mult).then_inc(mx_ready[3], 1)

            def turned3(g, c):
                dve.wait_ge(eT_done[3], QC * g.q + c + 2)
                dve.wait_ge(pv_done[3], g.q + 2)
                nc.vector.tensor_copy(eT[:, c, :, :], ps[:, 6, :].rearrange("p (h n) -> p h n", h=H)).then_inc(eT_outd, 1)

            def add_up3(g):
                q, b = g.q, g.b
                t = quad_value(dve, quad_tile, q, T)
                total = totals[3][:, bass.ds(t, 1), :].rearrange("p t h -> p (t h)")
                link = Link(dve, link_u, 2, q)
                dve.wait_ge(al_ready[3], q + 2)
                dve.wait_ge(e_ready[3], H * q + H + 2)
                settle(dve)
                nc.vector.tensor_copy(tops[3][:, bass.ds(t, 1), :].rearrange("p t h -> p (t h)"), best3[:, b, :])
                heads = acc[:, t, :].rearrange("p (h c) -> p h c", h=H)
                nc.vector.tensor_tensor(heads, heads, per_head(alpha3[:, b, :]), ALU.mult)
                link(nc.vector.tensor_tensor(total, total, alpha3[:, b, :], ALU.mult))
                link(nc.vector.tensor_tensor(total, total, part3[:, b, :], ALU.add))
                link.end()
                dve.wait_ge(o_done, q + 2)
                settle(dve)
                nc.vector.tensor_tensor(acc[:, t, :], acc[:, t, :], ps[:, 7, P:2 * P], ALU.add).then_inc(pv_read[3], 1)
                dve.wait_ge(pv_read[3], q + 3)
                settle(dve)

            def finish3(i):
                link = Link(dve, link_e[3], 15, i)
                tiles = bass.ds(FT * i, FT)
                o, dif, prod, more_prod = (fin[:, n, :, :] for n in range(4))
                own = xr[:, tiles, :]
                wide_wb = [wb_bc[:, n * P:(n + 1) * P].rearrange("p (a f) -> p a f", a=1).to_broadcast([P, FT, P])
                           for n in range(3)]
                link(nc.vector.tensor_scalar(rden[:, :, :], totals[3][:, tiles, :], TINY, None, ALU.max))
                link(nc.vector.reciprocal(rden[:, :, :], rden[:, :, :]))
                link(nc.vector.tensor_scalar(some[:, :, :], tops[3][:, tiles, :], 0.5 * LOW, None, ALU.is_gt))
                link(nc.vector.tensor_tensor(rden[:, :, :], rden[:, :, :], some[:, :, :], ALU.mult))
                link(nc.vector.tensor_tensor(o.rearrange("p t (c h) -> p t h c", h=H),
                                             acc[:, tiles, :].rearrange("p t (h c) -> p t h c", h=H),
                                             rden[:, :, :].rearrange("p t (h a) -> p t h a", a=1)
                                             .to_broadcast([P, FT, H, C]), ALU.mult))
                link(nc.vector.tensor_tensor(dif, o, own, ALU.subtract))
                nc.vector.tensor_tensor(prod, o, wide_wb[0], ALU.mult)
                link(nc.vector.tensor_tensor(more_prod, own, wide_wb[1], ALU.mult))
                link(nc.vector.tensor_tensor(prod, prod, more_prod, ALU.add))
                link(nc.vector.tensor_tensor(more_prod, dif, wide_wb[2], ALU.mult))
                link(nc.vector.tensor_tensor(prod, prod, more_prod, ALU.add))
                nc.vector.tensor_reduce(zed[:, :, 0:1].rearrange("p t a -> p (t a)"), prod, AX.X, ALU.add).then_inc(z_ready, 1)
                dve.wait_ge(ez_ready, i + 1)
                settle(dve)
                link(nc.vector.tensor_scalar(zed[:, :, :], zed[:, :, :], -1.0, -1.0, ALU.mult, ALU.add))
                link(nc.vector.reciprocal(zed[:, :, :], zed[:, :, :]))
                link(nc.vector.tensor_tensor(dif, dif, wide(zed[:, :, :]), ALU.mult))
                link(nc.vector.tensor_tensor(o, o, dif, ALU.add))
                link(nc.vector.tensor_tensor(x_sb[:, tiles, :], o, x_sb[:, tiles, :], ALU.add))
                link.end()

            def step3(g):
                mask3(g.ahead(1))
                scores(g.ahead(1), (0, 1))
                turned3(g, 1)
                scores(g.ahead(1), (2, 3))
                maxima3(g.ahead(1))
                turned3(g, 3)
                queries(g.ahead(2))
                add_up3(g)

            clear(3)
            nc.vector.memset(qT[:, T * P:(T + 1) * P], 0.0)
            queries(Quad(0, 0))
            mask3(Quad(0, 0))
            scores(Quad(0, 0), range(H))
            maxima3(Quad(0, 0))
            queries(Quad(0, 1))
            end = Quad(each_quad(dve, step3), 0)
            dve.wait_ge(e_ready[3], H * end.q + H + 2)
            settle(dve)
            with dve.Fori(0, T // FT) as i:
                finish3(i)

        @block.tensor
        def _(pe):
            mm = nc.tensor.matmul
            pe.wait_ge(cst, 7)
            pe.wait_ge(iotas, 13)
            pe.wait_ge(ld, 16 * NLD)

            def project(k):
                def add_rows(t, b):
                    pe.wait_ge(ht_ready[1], t + 1)
                    mm(ps[:, 6, 0:P], ones[:, :], h_t[:, b, 0:P], start=isinstance(t, int) and t == 0,
                       stop=False).then_inc(mean_done, 1)

                def turn(t, b):
                    pe.wait_ge(ht_ready[k], t + 1)
                    wait(pe, hT_ready[k], t - 1)
                    nc.tensor.transpose(ps[:, b, 0:P], h_t[:, b, 0:P], ident[:, :]).then_inc(tr_done[k], 1)

                def multiply(t, b):
                    pe.wait_ge(hT_ready[k], t + 1)
                    wait(pe, post_done[k], t - 1)
                    got = ps[:, 2 + b, 0:P]
                    if k == 0:
                        ins = mm(got, hT[:, b, :], k0_sb[:, :], start=True, stop=True)
                    elif k == 2:
                        ins = mm(got, hT[:, b, :], w2_sb[:, 0, :], start=True, stop=True)
                    else:
                        mm(ps[:, 2 + b, 0:3 * P], hT[:, b, :], wkvs_sb[:, :], start=True, stop=True)
                        ins = mm(ps[:, 4 + b, 0:P], wq_sb[:, :], hT[:, b, :], start=True, stop=True)
                    ins.then_inc(proj_done[k], 1)

                if k == 1:
                    each_tile(pe, add_rows)
                else:
                    overlapped(pe, turn, multiply)

            def places(nb):
                pe.wait_ge(flag_ready, nb + 3)
                pe.wait_ge(place_read, nb + 1)
                flags = flag[:, :, :].rearrange("p t m -> p (t m)")
                mm(ps[:, 5, 128:256], tri[:, :], flags, start=True, stop=True)
                mm(ps[:, 5, 256:384], ones_b[:, :], flags, start=True, stop=True).then_inc(place_done, 1)

            def a_list(nb, j):
                n = nb * TB + j
                pe.wait_ge(coded_ready, n + 1)
                pe.wait_ge(list_read, n + 1)
                for m in range(T):
                    ins = mm(ps[:, 7 if j % 2 else 3, 0:3 * NC], onehot[:, j % 2, :, m],
                             coded[:, j % 2, :, :, m].rearrange("p v c -> p (v c)"), start=(m == 0), stop=(m == T - 1))
                ins.then_inc(list_done, 1)

            def block0(nb, last):
                pe.wait_ge(agg_out, 1 + nb)
                if last is not None:
                    places(last)
                for q in range(NQ):
                    pe.wait_ge(slot_full[q], 16 * (nb + 1))
                    for m in range(MQ):
                        ins = mm(ps[:, 0, :], h_sb[:, q * MQ + m, :], ring[:, q, m, :],
                                 start=(q + m == 0), stop=(q * MQ + m == T - 1))
                    ins.then_inc(slot_used[q] if q < NQ - 1 else agg_done, 1)
                    if last is not None and q < NQ - 1:
                        a_list(last, q)
                for q in range(NQ):
                    pe.wait_ge(slot_summed[q], nb + 1)
                for j in range(TB):
                    for q in range(NQ):
                        ins = mm(ps[:, 6, j:j + 1], degp[:, q, j * P:(j + 1) * P], ones[:, 0:1],
                                 start=(q == 0), stop=(q == NQ - 1))
                ins.then_inc(deg_done, 1)
                pe.wait_ge(up_used, 1 + nb)
                pe.wait_ge(agg_out, nb + 2)
                for j in range(TB):
                    ins = mm(ps[:, 1, j * P:(j + 1) * P], aggT[:, j * P:(j + 1) * P], k0_sb[:, :], start=True, stop=True)
                ins.then_inc(up_done, 1)
                if last is not None:
                    a_list(last, NQ - 1)

            project(0)
            pe.wait_ge(ht_copied, T)
            pe.wait_ge(post_done[0], T)
            block0(0, None)
            with pe.Fori(1, NB) as nb:
                block0(nb, nb - 1)
            places(NB - 1)
            for j in range(TB):
                a_list(NB - 1, j)
            project(1)
            mm(ps[:, 6, 0:P], zeros[:, :], ident[:, :], start=False, stop=True).then_inc(mean_done, 1)
            for n in range(3):
                pe.wait_ge(qv_ready, n + 1)
                if n:
                    pe.wait_ge(link_q, 10 + n)
                mm(ps[:, 1, 0:3 * P], ones[:, :], qdiag[:, :, :].rearrange("p c n -> p (c n)"), start=True,
                   stop=True).then_inc(qv_done, 1)
            pe.wait_ge(tables_ready, 1)

            def logits(g):
                q, b = g.q, g.b
                pe.wait_ge(lgT_ready, q + 2)
                pe.wait_ge(e_ready[1], q + 1)
                for c in range(QC):
                    ins = nc.tensor.transpose(ps[:, b, c * P:(c + 1) * P], lgT[:, b, c, :], ident[:, :])
                ins.then_inc(lg_done, 1)

            def step1(g):
                q, b = g.q, g.b
                pe.wait_ge(e_ready[1], q + 3)
                pe.wait_ge(eT_out[1], q + 1)
                for c in range(QC):
                    ins = nc.tensor.transpose(ps[:, 3, c * P:(c + 1) * P], e1[:, b, c * P:(c + 1) * P], ident[:, :])
                ins.then_inc(eT_done[1], 1)
                logits(g.ahead(1))
                pe.wait_ge(eT_out[1], q + 2)
                pe.wait_ge(pv_read[1], q + 1)
                nodes_gathered(pe, 1, g)
                for c in range(QC):
                    ins = mm(ps[:, 4 + b, 0:P], eT[:, c, 0, :], hg1[:, b, c, 0:P], start=(c == 0), stop=(c == QC - 1))
                ins.then_inc(pv_done[1], 1)

            logits(Quad(0, 0))
            each_quad(pe, step1)

            project(2)
            pe.wait_ge(post_done[2], T)

            def neighbours(g):
                q, b = g.q, g.b
                adj_loaded(pe, 2, g)
                nodes_gathered(pe, 2, g)
                pe.wait_ge(pv_read[2], q + 1)
                for c in range(QC):
                    ins = mm(ps[:, b, 0:P], hg2[:, b, c, :], ac[:, b, c, :], start=(c == 0), stop=(c == QC - 1))
                ins.then_inc(pv_done[2], 1)

            def step2(g):
                neighbours(g.ahead(1))

            neighbours(Quad(0, 0))
            each_quad(pe, step2)
            with pe.Fori(0, NB) as nb:
                pe.wait_ge(agg_ready, nb + 2)
                pe.wait_ge(w_read, nb + 1)
                for j in range(TB):
                    ins = mm(ps[:, 3, j * P:(j + 1) * P], aggT[:, j * P:(j + 1) * P], w2_sb[:, 1, :], start=True, stop=True)
                ins.then_inc(w_done, 1)

            project(3)
            pe.wait_ge(post_done[3], T)

            def turn_rows(g):
                q, b = g.q, g.b
                nodes_gathered(pe, 3, g)
                pe.wait_ge(kT_out, q + 1)
                for c in range(QC):
                    ins = nc.tensor.transpose(ps[:, 0, c * P:(c + 1) * P], kvg[:, b, c, 0:P], ident[:, :])
                ins.then_inc(kT_done, 1)
                adj_loaded(pe, 3, g)
                pe.wait_ge(neg_ready, q + 1)
                for c in range(QC):
                    ins = nc.tensor.transpose(ps[:, 1, c * P:(c + 1) * P], ac[:, b, c, :], ident[:, :])
                ins.then_inc(agT_done, 1)

            def scores(g, heads):
                q, b = g.q, g.b
                pe.wait_ge(kT_out, q + 2)
                pe.wait_ge(qz_ready, q + 2)
                for h in heads:
                    pe.wait_ge(s_read, H * q + max(h - 2, 0) + 1)
                    mm(ps[:, 2 + h % 3, :], qz[:, b, h, :], kT[:, :], start=True, stop=True).then_inc(s_done, 1)

            def turn_exps(g, chunks):
                q, b = g.q, g.b
                pe.wait_ge(e_ready[3], H * q + H + 2)
                for c in chunks:
                    pe.wait_ge(eT_outd if c % 2 else eT_out[3], 2 * q + c // 2 + 1)
                    for h in range(H):
                        ins = nc.tensor.transpose(ps[:, 5 + c % 2, h * P:(h + 1) * P], e[:, b, h, c * P:(c + 1) * P],
                                                  ident[:, :])
                    ins.then_inc(eT_done[3], 1)

            def values(g):
                q, b = g.q, g.b
                pe.wait_ge(pv_read[3], q + 2)
                for h in range(H):
                    for c in range(QC):
                        if h == 0:
                            pe.wait_ge(eT_outd if c % 2 else eT_out[3], 2 * q + c // 2 + 2)
                        ins = mm(ps[C * h:C * h + C, 7, 0:P], kvg[:, b, c, P + C * h:P + C * h + C], eT[:, c, h, :],
                                 start=(c == 0), stop=(c == QC - 1))
                ins.then_inc(pv_done[3], 1)

            def step3(g):
                scores(g.ahead(1), (0, 1))
                turn_exps(g, (0, 1))
                scores(g.ahead(1), (2, 3))
                turn_exps(g, (2, 3))
                values(g)
                turn_rows(g.ahead(2))
                pe.wait_ge(oT_out, g.q + 2)
                nc.tensor.transpose(ps[:, 7, P:2 * P], outT[:, :], ident[:, :]).then_inc(o_done, 1)

            turn_rows(Quad(0, 0))
            scores(Quad(0, 0), range(H))
            turn_rows(Quad(0, 1))
            each_quad(pe, step3)


def kernel(**inputs):
    import concourse.bacc as bacc
    from concourse.bass_utils import run_bass_kernel_spmd

    i = {n: np.asarray(v) for n, v in inputs.items()}
    blocks = i["adj"].reshape(NB, TB, P, T, P).transpose(0, 4, 3, 1, 2).reshape(ZERO_ROW, P)
    blocks = np.concatenate([blocks, np.zeros((P, P), blocks.dtype)])
    arrays = {
        "x": i["x"], "adj_rows": blocks,
        "k0": i["L0_gnn_kernel"], "b0": i["L0_gnn_bias"], "beta": i["L0_gnn_beta"],
        "hv": i["L1_gnn_H_v"], "w2": np.ascontiguousarray(i["L2_gnn_W"].T), "b2": i["L2_gnn_b"],
        "wq": i["L3_gnn_Wq"], "bq": i["L3_gnn_bq"], "wk": i["L3_gnn_Wk"], "bk": i["L3_gnn_bk"],
        "wv": i["L3_gnn_Wv"], "bv": i["L3_gnn_bv"], "ws": i["L3_gnn_Ws"], "bs": i["L3_gnn_bs"],
        "wb": i["L3_gnn_Wb"],
    }
    nc = bacc.Bacc("TRN2", target_bir_lowering=False, num_devices=1)
    a = {n: nc.dram_tensor("in_" + n, v.shape, mybir.dt.from_np(v.dtype), kind="ExternalInput").ap()
         for n, v in arrays.items()}
    out = nc.dram_tensor("out_x", (N, P), F32, kind="ExternalOutput").ap()
    h1_table, h2_table, kv_table, adj_table = (
        nc.dram_tensor(n, shape, F32, kind="Internal").ap()
        for n, shape in (("h1_table", (N + 1, P + 1)), ("h2_table", (N + 1, P)), ("kv_table", (N + 1, 2 * P)),
                         ("adj_table", ((QUADS + BEHIND + 1) * P, QW))))
    build(nc, a["x"], a["adj_rows"], a["k0"], a["b0"], a["beta"], a["hv"], a["w2"], a["b2"],
          a["wq"], a["bq"], (a["wk"], a["wv"], a["ws"]), (a["bk"], a["bv"], a["bs"]), a["wb"], out, h1_table, h2_table, kv_table, adj_table)
    r = run_bass_kernel_spmd(nc, [{"in_" + n: np.ascontiguousarray(v) for n, v in arrays.items()}], core_ids=[0])
    return r.results[0]["out_x"]
```
